# Optimizing a Trainium2 kernel written in Bass

```python
import numpy as np
import jax
import jax.numpy as jnp

def _softmax(x, axis=-1):
    return jax.nn.softmax(x, axis=axis)

def _gelu(x):
    return jax.nn.gelu(x, approximate=True)

def _silu(x):
    return jax.nn.silu(x)

def _sigmoid(x):
    return jax.nn.sigmoid(x)

def _layernorm(x, axis=-1, eps=1e-05):
    m = jnp.mean(x, axis=axis, keepdims=True)
    v = jnp.var(x, axis=axis, keepdims=True)
    return (x - m) / jnp.sqrt(v + eps)

def _scatter_add(tgt, idx, src, axis=0):
    return tgt.at[idx].add(src)

def _segment_sum(src, seg, n):
    return jax.ops.segment_sum(src, seg, n)
kernel_name = 'mk_recurrent_d1_jaxref_r8_e82348'

def setup_inputs(seed: int=0):
    np.random.seed(seed)
    _w = jnp.asarray

    def _L0_attn_setup():
        import jax, jax.numpy as jnp
        import numpy as np
        BSZ, T, D, H, WIN, N = (2, 256, 128, 16, 128, 64)
        DH = D // H
        DFF = 4 * D

        def _layernorm(x, g, b, eps=1e-05):
            mu = jnp.mean(x, axis=-1, keepdims=True)
            var = jnp.mean((x - mu) ** 2, axis=-1, keepdims=True)
            return (x - mu) * jax.lax.rsqrt(var + eps) * g + b
        key = jax.random.key(seed)
        ks = jax.random.split(key, 16)
        w = lambda k, shape: (jax.random.normal(k, shape) * 0.02).astype(jnp.float32)
        return {'x': jax.random.normal(ks[0], (BSZ, T, D), dtype=jnp.float32), 'ln1_g': jnp.ones((D,), jnp.float32), 'ln1_b': jnp.zeros((D,), jnp.float32), 'WQ': w(ks[1], (D, D)), 'bQ': jnp.zeros((D,), jnp.float32), 'WK': w(ks[2], (D, D)), 'bK': jnp.zeros((D,), jnp.float32), 'WV': w(ks[3], (D, D)), 'bV': jnp.zeros((D,), jnp.float32), 'WO': w(ks[4], (D, D)), 'bO': jnp.zeros((D,), jnp.float32), 'Wg': w(ks[5], (D, D)), 'bg': jnp.zeros((D,), jnp.float32), 'A': jax.random.uniform(ks[6], (N,), jnp.float32, -0.1, 0.1), 'Bw': w(ks[7], (D, N)), 'Cw': w(ks[8], (N, D)), 'ln2_g': jnp.ones((D,), jnp.float32), 'ln2_b': jnp.zeros((D,), jnp.float32), 'W1': w(ks[9], (D, DFF)), 'b1': jnp.zeros((DFF,), jnp.float32), 'W2': w(ks[10], (DFF, D)), 'b2': jnp.zeros((D,), jnp.float32)}
    _L0_attn_in = _L0_attn_setup()

    def _L0_ffn_setup():
        import jax, jax.numpy as jnp
        import numpy as np
        B, S, H, I, E, K = (4, 256, 128, 128, 8, 2)
        LIMIT = 7.0
        ALPHA = 1.702
        EPS = 1e-05
        key = jax.random.key(seed)
        ks = jax.random.split(key, 5)
        x = jax.random.normal(ks[0], (B, S, H), dtype=jnp.float32)
        norm_weight = jnp.ones((H,), dtype=jnp.float32)
        gate_weight = (jax.random.normal(ks[1], (E, H), dtype=jnp.float32) / np.sqrt(H)).astype(jnp.bfloat16)
        gate_bias = jnp.zeros((E,), dtype=jnp.bfloat16)
        mlp1_weight = (jax.random.normal(ks[2], (E, 2 * I, H), dtype=jnp.float32) / np.sqrt(H)).astype(jnp.bfloat16)
        mlp1_bias = jnp.zeros((E, 2 * I), dtype=jnp.bfloat16)
        mlp2_weight = (jax.random.normal(ks[3], (E, H, I), dtype=jnp.float32) / np.sqrt(I)).astype(jnp.bfloat16)
        mlp2_bias = jnp.zeros((E, H), dtype=jnp.bfloat16)
        return {'x': x, 'norm_weight': norm_weight, 'gate_weight': gate_weight, 'gate_bias': gate_bias, 'mlp1_weight': mlp1_weight, 'mlp1_bias': mlp1_bias, 'mlp2_weight': mlp2_weight, 'mlp2_bias': mlp2_bias}
    _L0_ffn_in = _L0_ffn_setup()
    _d = {'L0_attn_x': _L0_attn_in['x'], 'L0_attn_ln1_g': _L0_attn_in['ln1_g'], 'L0_attn_ln1_b': _L0_attn_in['ln1_b'], 'L0_attn_WQ': _L0_attn_in['WQ'], 'L0_attn_bQ': _L0_attn_in['bQ'], 'L0_attn_WK': _L0_attn_in['WK'], 'L0_attn_bK': _L0_attn_in['bK'], 'L0_attn_WV': _L0_attn_in['WV'], 'L0_attn_bV': _L0_attn_in['bV'], 'L0_attn_WO': _L0_attn_in['WO'], 'L0_attn_bO': _L0_attn_in['bO'], 'L0_attn_Wg': _L0_attn_in['Wg'], 'L0_attn_bg': _L0_attn_in['bg'], 'L0_attn_A': _L0_attn_in['A'], 'L0_attn_Bw': _L0_attn_in['Bw'], 'L0_attn_Cw': _L0_attn_in['Cw'], 'L0_attn_ln2_g': _L0_attn_in['ln2_g'], 'L0_attn_ln2_b': _L0_attn_in['ln2_b'], 'L0_attn_W1': _L0_attn_in['W1'], 'L0_attn_b1': _L0_attn_in['b1'], 'L0_attn_W2': _L0_attn_in['W2'], 'L0_attn_b2': _L0_attn_in['b2'], 'L0_ffn_norm_weight': _L0_ffn_in['norm_weight'], 'L0_ffn_gate_weight': _L0_ffn_in['gate_weight'], 'L0_ffn_gate_bias': _L0_ffn_in['gate_bias'], 'L0_ffn_mlp1_weight': _L0_ffn_in['mlp1_weight'], 'L0_ffn_mlp1_bias': _L0_ffn_in['mlp1_bias'], 'L0_ffn_mlp2_weight': _L0_ffn_in['mlp2_weight'], 'L0_ffn_mlp2_bias': _L0_ffn_in['mlp2_bias']}
    _x0 = _d['L0_attn_x']
    _d['L0_attn_x'] = jax.random.normal(jax.random.fold_in(jax.random.key(seed), 1), (16, 512, 128), dtype=_x0.dtype)
    del _x0
    return _d

def reference(L0_attn_x, L0_attn_ln1_g, L0_attn_ln1_b, L0_attn_WQ, L0_attn_bQ, L0_attn_WK, L0_attn_bK, L0_attn_WV, L0_attn_bV, L0_attn_WO, L0_attn_bO, L0_attn_Wg, L0_attn_bg, L0_attn_A, L0_attn_Bw, L0_attn_Cw, L0_attn_ln2_g, L0_attn_ln2_b, L0_attn_W1, L0_attn_b1, L0_attn_W2, L0_attn_b2, L0_ffn_norm_weight, L0_ffn_gate_weight, L0_ffn_gate_bias, L0_ffn_mlp1_weight, L0_ffn_mlp1_bias, L0_ffn_mlp2_weight, L0_ffn_mlp2_bias):

    def _L0_attn_ref(x, ln1_g, ln1_b, WQ, bQ, WK, bK, WV, bV, WO, bO, Wg, bg, A, Bw, Cw, ln2_g, ln2_b, W1, b1, W2, b2):
        import jax, jax.numpy as jnp
        import numpy as np
        BSZ, T, D, H, WIN, N = (2, 256, 128, 16, 128, 64)
        DH = D // H
        DFF = 4 * D

        def _layernorm(x, g, b, eps=1e-05):
            mu = jnp.mean(x, axis=-1, keepdims=True)
            var = jnp.mean((x - mu) ** 2, axis=-1, keepdims=True)
            return (x - mu) * jax.lax.rsqrt(var + eps) * g + b
        B, Tlen, d = x.shape
        h = _layernorm(x, ln1_g, ln1_b)

        def heads(t):
            return t.reshape(B, Tlen, H, DH).transpose(0, 2, 1, 3)
        q = heads(h @ WQ + bQ)
        k = heads(h @ WK + bK)
        v = heads(h @ WV + bV)
        scores = jnp.einsum('bhqd,bhkd->bhqk', q, k) / jnp.sqrt(jnp.float32(DH))
        i = jnp.arange(Tlen)
        diff = i[:, None] - i[None, :]
        allowed = (diff >= 0) & (diff < WIN)
        scores = jnp.where(allowed, scores, -jnp.inf)
        attn = jax.nn.softmax(scores, axis=-1)
        ao = jnp.einsum('bhqk,bhkd->bhqd', attn, v)
        ao = ao.transpose(0, 2, 1, 3).reshape(B, Tlen, d)
        attn_out = ao @ WO + bO
        u = h @ Bw

        def step(s, u_t):
            s = A * s + u_t
            return (s, s)
        _, states = jax.lax.scan(step, jnp.zeros((B, N), x.dtype), jnp.swapaxes(u, 0, 1))
        ssm_out = jnp.swapaxes(states, 0, 1) @ Cw
        g = jax.nn.sigmoid(h @ Wg + bg)
        x1 = x + g * attn_out + (1.0 - g) * ssm_out
        h2 = _layernorm(x1, ln2_g, ln2_b)
        mlp = jax.nn.gelu(h2 @ W1 + b1, approximate=False) @ W2 + b2
        return x1 + mlp

    def _L0_ffn_ref(x, norm_weight, gate_weight, gate_bias, mlp1_weight, mlp1_bias, mlp2_weight, mlp2_bias):
        import jax, jax.numpy as jnp
        import numpy as np
        B, S, H, I, E, K = (4, 256, 128, 128, 8, 2)
        LIMIT = 7.0
        ALPHA = 1.702
        EPS = 1e-05
        xc = x.astype(jnp.bfloat16)
        xf = xc.astype(jnp.float32)
        rms = jnp.mean(xf * xf, axis=-1, keepdims=True)
        normed = (xf * jax.lax.rsqrt(rms + EPS) * norm_weight).astype(jnp.bfloat16)
        nf = normed.astype(jnp.float32)
        logits = (jnp.einsum('bsh,eh->bse', nf, gate_weight.astype(jnp.float32)) + gate_bias.astype(jnp.float32)).astype(jnp.bfloat16).astype(jnp.float32)
        scores, idx = jax.lax.top_k(logits, K)
        w = jax.nn.softmax(scores, axis=-1)
        combine = jnp.sum(jax.nn.one_hot(idx, E, dtype=jnp.float32) * w[..., None], axis=-2)
        p1 = jnp.einsum('bsh,eoh->bseo', nf, mlp1_weight.astype(jnp.float32)) + mlp1_bias.astype(jnp.float32)
        g = jnp.minimum(p1[..., 0::2], LIMIT)
        lin = jnp.clip(p1[..., 1::2], -LIMIT, LIMIT)
        act = g * jax.nn.sigmoid(ALPHA * g) * (lin + 1.0)
        p2 = jnp.einsum('bsei,ehi->bseh', act, mlp2_weight.astype(jnp.float32)) + mlp2_bias.astype(jnp.float32)
        combined = jnp.einsum('bseh,bse->bsh', p2, combine)
        out = (xc + combined.astype(jnp.bfloat16)).astype(x.dtype)
        return out
    x = L0_attn_x
    xn = _layernorm(x, axis=-1)
    s = _L0_attn_ref(xn, L0_attn_ln1_g, L0_attn_ln1_b, L0_attn_WQ, L0_attn_bQ, L0_attn_WK, L0_attn_bK, L0_attn_WV, L0_attn_bV, L0_attn_WO, L0_attn_bO, L0_attn_Wg, L0_attn_bg, L0_attn_A, L0_attn_Bw, L0_attn_Cw, L0_attn_ln2_g, L0_attn_ln2_b, L0_attn_W1, L0_attn_b1, L0_attn_W2, L0_attn_b2)
    g = _silu(_L0_ffn_ref(xn, L0_ffn_norm_weight, L0_ffn_gate_weight, L0_ffn_gate_bias, L0_ffn_mlp1_weight, L0_ffn_mlp1_bias, L0_ffn_mlp2_weight, L0_ffn_mlp2_bias))
    x = x + s * g
    return x

_drawn_inputs = setup_inputs


def setup_inputs(seed=0):
    import zlib

    import numpy as np

    out = dict(_drawn_inputs(seed))
    spreads = {'L0_attn_ln1_g': (1.0, 0.6),
     'L0_attn_ln1_b': (0.0, 0.8),
     'L0_attn_bQ': (0.0, 0.8),
     'L0_attn_bK': (0.0, 2.0),
     'L0_attn_bV': (0.0, 0.8),
     'L0_attn_bO': (0.0, 0.389),
     'L0_attn_bg': (0.0, 0.8),
     'L0_attn_ln2_g': (1.0, 0.6),
     'L0_attn_ln2_b': (0.0, 2.0),
     'L0_attn_b1': (0.0, 0.8),
     'L0_attn_b2': (0.0, 0.393),
     'L0_ffn_norm_weight': (1.0, 0.2),
     'L0_ffn_gate_bias': (0.0, 0.1),
     'L0_ffn_mlp1_bias': (0.0, 0.1),
     'L0_ffn_mlp2_bias': (0.0, 0.286)}
    factors = {'L0_attn_WQ': 8.0,
     'L0_attn_WK': 8.0,
     'L0_attn_WV': 8.0,
     'L0_attn_WO': 8.0,
     'L0_attn_Wg': 8.0,
     'L0_attn_A': 8.0,
     'L0_attn_Bw': 7.75,
     'L0_attn_Cw': 7.64,
     'L0_attn_W1': 2.667}
    for name, (base, spread) in spreads.items():
        noise = np.random.default_rng([zlib.crc32(name.encode()), seed]).standard_normal(out[name].shape)
        drawn = base * np.exp(spread * noise) if base else spread * noise
        out[name] = jnp.asarray(drawn.astype(out[name].dtype))
    for name, factor in factors.items():
        out[name] = (out[name] * factor).astype(out[name].dtype)
    return out
```

```python
from contextlib import ExitStack

import numpy as np

import concourse.bass as bass
from concourse import mybir

ALU = mybir.AluOpType
ACT = mybir.ActivationFunctionType
AX = mybir.AxisListType
F32 = mybir.dt.float32
BF16 = mybir.dt.bfloat16

B, T, D = 16, 512, 128
P = 128
NT = T // P
H, DH = 16, 8
NPAIR = H // 2
HG = 4
NG = H // HG
NCH = NG * NT
N = 64
DFF = 512
NJ = DFF // P
E, I = 8, 128
VW = 32
NPART = 3
SHIFT = 6 * DH
EPS = 1e-5
LIMIT, ALPHA = 7.0, 1.702
G_LIMIT = float(LIMIT / (1.0 + np.exp(-ALPHA * LIMIT)))
SCALE = float(1.0 / np.sqrt(np.float32(DH)))
NEG = -1e30
TIE = -1e-37
CONSTS = 4


class Signal:

    def __init__(self, sem, per):
        self.sem, self.per = sem, per


def build(nc, a, out):
    with ExitStack() as ctx:
        def sb(name, shape, dt=F32):
            return ctx.enter_context(nc.sbuf_tensor(name, shape, dt))

        def signal(name, per):
            return Signal(ctx.enter_context(nc.semaphore(name)), per)

        ps = ctx.enter_context(nc.psum_tensor("ps", [P, 8, 512], F32))

        def bank(k):
            return ps[:, k, :]

        def bank_t(k):
            return ps[:, k, :].rearrange("p (t d) -> p t d", t=NT)

        def bank_bf(k):
            return ps[:, k, :].bitcast(BF16)[:, 0:T]

        ident = sb("ident", [P, P])
        identb = sb("identb", [P, P], BF16)
        mask = sb("mask", [P, 2, 2 * P], BF16)
        sel = sb("sel", [P, E, P], BF16)
        tie = sb("tie", [P, E, E])
        half = sb("half", [P, NT])
        zrow = sb("zrow", [NPART, T], BF16)
        wq, wk, wv, wo, wg = (sb(n, [P, P]) for n in ("wq", "wk", "wv", "wo", "wg"))
        bw = sb("bw", [P, P])
        cw = sb("cw", [P, P])
        ncw = sb("ncw", [P, P])
        w1 = sb("w1", [P, DFF])
        w2 = sb("w2", [P, NJ, P])
        cols = {n: sb(n, [P, 1]) for n in ("ln1_g", "ln1_b", "bQ", "bK", "ln2_g", "ln2_b")}
        b1c = sb("b1c", [P, NJ])
        acol = sb("acol", [P, 1])
        rows = {n: sb("row_" + n, [P, P]) for n in ("bV", "bg", "b2", "nw")}
        gbias_b = sb("gbias_b", [P, E], BF16)
        gbias = sb("gbias", [P, E])
        gw = sb("gw", [P, E], BF16)
        m1 = sb("m1", [P, E, 2, P], BF16)
        m2 = sb("m2", [P, E, P])
        mb_b = sb("mb_b", [P, E, 2], BF16)
        mbias = sb("mbias", [P, E, 2])
        b2st = sb("b2st", [P, P], BF16)

        xl = sb("xl", [P, 2, NT, D])
        stats = sb("stats", [P, NT, 6])
        mv = sb("mv", [P, NT, 2])
        r1, r1t, vv, r2, sq, sqm, rs = (sb(n, [P, NT]) for n in ("r1", "r1t", "vv", "r2", "sq", "sqm", "rs"))
        vt = sb("vt", [P, NT])
        xn = sb("xn", [P, 2, NT, D])
        xc = sb("xc", [P, 2, NT, D], BF16)
        junk = sb("junk", [P, NT, D], BF16)
        h0 = sb("h0", [P, NT, D])
        nf = sb("nf", [P, NT, D], BF16)
        hT = sb("hT", [P, T])
        nfT = sb("nfT", [P, 2, T], BF16)
        qp = sb("qp", [P, NPART, T], BF16)
        kp = sb("kp", [P, NPART, T], BF16)
        qr = sb("qr", [P, T])
        kr = sb("kr", [P, T])
        qz = [sb(f"qz{i}", [P, NPAIR, 2, T], BF16) for i in range(2)]
        kd = [sb(f"kd{i}", [P, NPAIR, T], BF16) for i in range(2)]
        va = sb("va", [P, 2, NT, H, VW])
        st = sb("st", [P, 2, T])
        gpre = sb("gpre", [P, NT, D])
        gth = sb("gth", [P, 2, NT, D])
        mx = sb("mx", [P, NT, H])
        mr = sb("mr", [P, NT, H])
        nm = sb("nm", [P, NT, NPART, H], BF16)
        nmT = sb("nmT", [NPART * H, T], BF16)
        NPT = 4
        pt = sb("pt", [P, NPT, HG, 2 * P])
        m1raw = pt[:, 0].rearrange("p h q -> p (h q)").bitcast(BF16).rearrange("p (e s h) -> p e s h", e=E, s=2)
        m2raw = pt[:, 1].rearrange("p h q -> p (h q)").bitcast(BF16)[:, 0:E * P].rearrange("p (e i) -> p e i", e=E)
        ot = sb("ot", [P, T])
        rz = sb("rz", [P, NT, HG])
        ao = sb("ao", [P, NT, H * DH])
        aoT = sb("aoT", [P, T])
        lg = sb("lg", [P, NT, E], BF16)
        dl = sb("dl", [P, NT, E, E])
        bt = sb("bt", [P, NT, E, E])
        rank = sb("rank", [P, NT, E])
        lmax = sb("lmax", [P, NT])
        ld = sb("ld", [P, NT, E])
        ex = sb("ex", [P, NT, E])
        exs = sb("exs", [P, NT, E])
        zs = sb("zs", [P, NT])
        zr = sb("zr", [P, NT])
        cmb = sb("cmb", [P, NT, E])
        cr = sb("cr", [P, NT, E])
        cp = sb("cp", [P, NT, P], BF16)
        cT = sb("cT", [P, 2, T], BF16)
        xnr = sb("xnr", [P, NT, D])
        xcr = sb("xcr", [P, NT, D], BF16)
        xr = sb("xr", [P, NT, D])
        t1 = sb("t1", [P, NT, D])
        s1 = sb("s1", [P, NT, D])
        x1 = sb("x1", [P, NT, D])
        x1b = sb("x1b", [P, NT, D])
        st2 = sb("st2", [P, NT, 6])
        mv2 = sb("mv2", [P, NT, 2])
        v2t = sb("v2t", [P, NT])
        r3 = sb("r3", [P, NT])
        h2 = sb("h2", [P, NT, D])
        h2T = sb("h2T", [P, T])
        hid = sb("hid", [P, NJ, T])
        sres = sb("sres", [P, NT, D])
        ga = sb("ga", [P, 2, T])
        lin = sb("lin", [P, 2, T])
        gc = sb("gc", [P, 2, T])
        act_t = sb("act_t", [P, 2, T])
        cb = sb("cb", [P, NT, D], BF16)
        z = sb("z", [P, NT, D], BF16)
        zth = sb("zth", [P, NT, D])
        w = sb("w", [P, NT, D])
        ob = sb("ob", [P, NT, D])

        blank_set = signal("blank_set", 1)
        pool_set = signal("pool_set", 1)
        weights_in = signal("weights_in", 1)
        pad_in = signal("pad_in", 1)
        expert_ps = signal("expert_ps", 1)
        expert_sb = signal("expert_sb", 1)
        consts = signal("consts", 1)
        x_in = signal("x_in", 16)
        xr_in = signal("xr_in", 16)
        xn_copied = signal("xn_copied", 16)
        xc_copied = signal("xc_copied", 16)
        stacks_in = signal("stacks_in", 16 * 6)
        qk_out = signal("qk_out", 16 * 6)
        nm_out = signal("nm_out", 16)
        shift_in = signal("shift_in", 16 * 2)
        out_st = signal("out_st", 16)
        stats_ok = signal("stats_ok", 1)
        mv_ok = signal("mv_ok", 1)
        r1_step = signal("r1_step", 2)
        r2_step = signal("r2_step", 4)
        xn_ok = signal("xn_ok", 1)
        xc_ok = signal("xc_ok", 1)
        sq_ok = signal("sq_ok", 1)
        rs_step = signal("rs_step", 2)
        h0_ok = signal("h0_ok", 1)
        nf_ok = signal("nf_ok", 1)
        hT_ps = signal("hT_ps", 1)
        hT_ok = signal("hT_ok", 1)
        q_ps = signal("q_ps", 1)
        k_ps = signal("k_ps", 1)
        v_ps = signal("v_ps", 1)
        u_ps = signal("u_ps", 1)
        g_ps = signal("g_ps", 1)
        qkhi_ok = signal("qkhi_ok", 2)
        qkr_ok = signal("qkr_ok", 2)
        qkmid_ok = signal("qkmid_ok", 2)
        qklo_ok = signal("qklo_ok", 2)
        v_ok = signal("v_ok", 1)
        st_ok = signal("st_ok", 1)
        gpre_ok = signal("gpre_ok", 1)
        gth_ok = signal("gth_ok", 1)
        s_ps = signal("s_ps", NCH)
        mx_ok = signal("mx_ok", NCH)
        nm_step = signal("nm_step", 4)
        nm_ps = signal("nm_ps", 1)
        nmT_ok = signal("nmT_ok", 1)
        sT_ps = signal("sT_ps", NCH)
        exp_ok = signal("exp_ok", NCH)
        pt_ok = signal("pt_ok", NCH)
        pv_ps = signal("pv_ps", NCH)
        ot_ok = signal("ot_ok", NG)
        ott_ps = signal("ott_ps", NG)
        rz_ok = signal("rz_ok", NG)
        ao_ok = signal("ao_ok", NG)
        aoT_ps = signal("aoT_ps", 1)
        aoT_ok = signal("aoT_ok", 1)
        wo_ps = signal("wo_ps", 1)
        cw_ps = signal("cw_ps", 1)
        t1_ok = signal("t1_ok", 1)
        s1_ok = signal("s1_ok", 1)
        x1_ok = signal("x1_ok", 1)
        x1b_ok = signal("x1b_ok", 1)
        st2_ok = signal("st2_ok", 1)
        mv2_ok = signal("mv2_ok", 1)
        r3_step = signal("r3_step", 2)
        h2_ok = signal("h2_ok", 1)
        h2T_ps = signal("h2T_ps", 1)
        h2T_ok = signal("h2T_ok", 1)
        w1_ps = signal("w1_ps", NJ)
        hid_ok = signal("hid_ok", NJ)
        w2_ps = signal("w2_ps", 1)
        s_ok = signal("s_ok", 1)
        nfT_ps = signal("nfT_ps", 1)
        nfT_ok = signal("nfT_ok", 1)
        lg_ps = signal("lg_ps", 1)
        lg_ok = signal("lg_ok", 1)
        route = signal("route", 12)
        ex_ok = signal("ex_ok", 1)
        cT_ps = signal("cT_ps", 1)
        cT_ok = signal("cT_ok", 1)
        up_ps = signal("up_ps", E)
        ga_ok = signal("ga_ok", E)
        lin_ok = signal("lin_ok", E)
        gc_ok = signal("gc_ok", E)
        act_ok = signal("act_ok", E)
        down_ps = signal("down_ps", E)
        cb_ok = signal("cb_ok", 1)
        z_ok = signal("z_ok", 1)
        zth_ok = signal("zth_ok", 1)
        y_ok = signal("y_ok", 1)
        w_ok = signal("w_ok", 1)
        ob_ok = signal("ob_ok", 1)

        spare = {}

        def apart(eng, b):
            if not isinstance(b, int):
                eng.sem_inc(spare[eng], 1)

        def set_spare(eng, name):
            spare[eng] = ctx.enter_context(nc.semaphore(name))

        def done(signal, batch, count=None):
            value = batch * signal.per + (signal.per if count is None else count)
            if isinstance(value, int) and value <= 0:
                return consts.sem, CONSTS
            return signal.sem, value

        x_d = a["x"].rearrange("b (t p) d -> b p t d", p=P)
        o_d = out.rearrange("b (t p) d -> b p t d", p=P)

        def row_of(v):
            return v.rearrange("(o d) -> o d", o=1).broadcast_to([P, v.shape[0]])

        def col_of(v, n=1):
            return v.rearrange("(j p) -> p j", j=n)

        WEIGHTS = [
            (wq[:], a["WQ"]), (wk[:], a["WK"]), (wv[:], a["WV"]), (wo[:], a["WO"]), (wg[:], a["Wg"]),
            (w1[:], a["W1"]), (w2[:], a["W2"].rearrange("(j p) d -> p j d", j=NJ)),
            *((cols[n][:], col_of(a[n])) for n in cols),
            (b1c[:], col_of(a["b1"], NJ)), (acol[0:N, :], col_of(a["A"])),
            (rows["bV"][:], row_of(a["bV"])), (rows["bg"][:], row_of(a["bg"])),
            (rows["b2"][:], row_of(a["b2"])), (rows["nw"][:], row_of(a["norm_weight"])),
            (gbias_b[:], row_of(a["gate_bias"])), (gw[:], a["gate_weight"].rearrange("e h -> h e")),
            (m1raw[:], a["mlp1_weight"].rearrange("e (i s) h -> i e s h", s=2)),
            (m2raw[:], a["mlp2_weight"].rearrange("e h i -> h e i")),
            (mb_b[:], a["mlp1_bias"].rearrange("e (i s) -> i e s", s=2)),
        ]
        PADDED = [
            (bw[:, 0:N], a["Bw"]), (cw[0:N, :], a["Cw"]),
            (ncw[N:N + 1, :], a["bO"].rearrange("(o d) -> o d", o=1)),
            *((b2st[E * c:E * (c + 1), :], a["mlp2_bias"]) for c in range(NPART)),
        ]
        BLANKS = [
            (mask[:], 0.0), (sel[:], 0.0), (tie[:], 0.0), (half[:], -0.5), (zrow[:], 0.0),
            (ident[:], 0.0), (identb[:], 0.0), (bw[:], 0.0), (cw[:], 0.0), (ncw[:], 0.0), (b2st[:], 0.0),
            (st[:], 0.0), (va[:], 0.0), (cp[:], 0.0), *((q[:], 0.0) for q in qz),
        ]
        ONES = [
            *((k[32 * r:32 * (r + 1)], 1.0) for k in kd for r in (1, 3)),
            (st[N:N + 1], 1.0), *((va[:, i, :, :, DH:DH + 1], 1.0) for i in range(2)),
        ]

        qk_d = nc.dram_tensor("qk_parts", (2, P, 6, T), BF16, kind="Internal").ap()
        nm_d = nc.dram_tensor("minus_maxima", (NPART * H, T), BF16, kind="Internal").ap()

        def at(tensor, b):
            return tensor[b] if isinstance(b, int) else tensor[bass.ds(b, 1)].rearrange("o p t d -> (o p) t d")

        block = ctx.enter_context(nc.Block())

        def schedule(eng, body):
            for b in range(-2, 2):
                body(b, b % 2)
            with eng.Fori(1, B // 2 - 1) as pair:
                body(2 * pair, 0)
                body(2 * pair + 1, 1)
            for b in range(B - 2, B + 1):
                body(b, b % 2)

        def has(b, lo=0):
            return not isinstance(b, int) or lo <= b < B

        def all_set(eng):
            for s, n in ((blank_set, len(BLANKS) + len(ONES)), (pool_set, 9), (weights_in, 16 * len(WEIGHTS)),
                         (pad_in, 16 * len(PADDED)), (expert_sb, 6), (consts, CONSTS)):
                eng.wait_ge(s.sem, n)

        @block.sync
        def _(sp):
            for dst, src in WEIGHTS:
                sp.dma_start(dst, src, allow_slow_non_contiguous=True).then_inc(weights_in.sem, 16)
            sp.wait_ge(blank_set.sem, len(BLANKS))
            for dst, src in PADDED:
                sp.dma_start(dst, src).then_inc(pad_in.sem, 16)
            all_set(sp)

            def body(b, q):
                if has(b + 2):
                    sp.wait_ge(*done(xn_ok, b))
                    sp.dma_start(xl[:, q], at(x_d, b + 2)).then_inc(x_in.sem, 16)
                if has(b - 1):
                    sp.wait_ge(*done(ob_ok, b - 1))
                    sp.dma_start(at(o_d, b - 1), ob[:]).then_inc(out_st.sem, 16)
                if has(b):
                    sp.dma_start(xr[:], at(x_d, b)).then_inc(xr_in.sem, 16)
                if has(b + 1):
                    sp.wait_ge(*done(nmT_ok, b + 1))
                    sp.wait_ge(*done(shift_in, b))
                    sp.dma_start(nm_d, nmT[:]).then_inc(nm_out.sem, 16)
                if has(b + 2):
                    sp.wait_ge(*done(stacks_in, b + 1))
                    for n, parts in enumerate((qp, kp)):
                        sp.wait_ge(*done(qklo_ok, b + 2, n + 1))
                        for first, count in ((0, 3), (3, 2), (5, 1)):
                            src = parts[:, 0:count] if n else \
                                parts[:, 3 - count:4 - count].to_broadcast([P, count, T])
                            sp.dma_start(qk_d[n, :, first:first + count], src).then_inc(qk_out.sem, 16)
                if has(b + 1):
                    sp.wait_ge(*done(nm_out, b + 1))
                    for par in range(2):
                        sp.dma_start(qz[1 - q][64 * par + SHIFT:64 * par + SHIFT + NPART, :, par],
                                     nm_d.rearrange("(r p two) t -> two r p t", r=NPART, two=2)[par]).then_inc(shift_in.sem, 16)
                if has(b + 2):
                    sp.wait_ge(*done(sT_ps, b))
                    sp.wait_ge(*done(qk_out, b + 2))
                    for par in range(2):
                        first = 64 * par
                        sp.dma_start(qz[q][first + SHIFT:first + SHIFT + NPART, :, par],
                                     zrow[:].unsqueeze(1).to_broadcast([NPART, NPAIR, T])).then_inc(stacks_in.sem, 16)
                        for n, dst in enumerate((qz[q][first:first + SHIFT, :, par], kd[q][first:first + SHIFT])):
                            src = qk_d[n].rearrange("(p two d) c t -> two (d c) p t", two=2, d=DH)[par]
                            sp.dma_start(dst, src).then_inc(stacks_in.sem, 16)
                if has(b + 1):
                    sp.wait_ge(*done(xn_ok, b + 1))
                    sp.wait_ge(*done(x1_ok, b))
                    sp.dma_start(xnr[:], xn[:, 1 - q]).then_inc(xn_copied.sem, 16)
                    sp.wait_ge(*done(xc_ok, b + 1))
                    sp.wait_ge(*done(z_ok, b))
                    sp.dma_start(xcr[:], xc[:, 1 - q]).then_inc(xc_copied.sem, 16)

            schedule(sp, body)
            sp.wait_ge(*done(out_st, B - 1))

        @block.tensor
        def _(pe):
            pe.wait_ge(blank_set.sem, len(BLANKS) + len(ONES))
            pe.wait_ge(pool_set.sem, 9)
            pe.wait_ge(weights_in.sem, 16 * len(WEIGHTS))
            for k in range(6):
                for c in range(4):
                    if k < 4:
                        src = m1raw[:, 2 * k + c // 2, c % 2, :]
                    else:
                        src = m2raw[:, 4 * (k - 4) + c, :]
                    mm = nc.tensor.transpose(bank_bf(k)[:, P * c:P * (c + 1)], src, identb[:])
                mm.then_inc(expert_ps.sem, 1)
            all_set(pe)

            def score_t(b, q, n):
                g, j = n // NT, n % NT
                if n == 0:
                    pe.wait_ge(*done(stacks_in, b))
                    pe.wait_ge(*done(shift_in, b))
                if n >= 2:
                    pe.wait_ge(*done(exp_ok, b, n - 1))
                else:
                    pe.wait_ge(*done(hid_ok, b - 1))
                    if has(b + 1):
                        for s in (nfT_ok, st_ok, qkr_ok, v_ok):
                            pe.wait_ge(*done(s, b + 1))
                w_q = 2 * P if j < NT - 1 else P
                for pr in range(2):
                    p = 2 * g + pr
                    o = bank(2 * (n % 2) + pr).rearrange("p (r q) -> p r q", r=2)[:, :, 0:w_q]
                    mm = nc.tensor.matmul(o, kd[q][:, p, P * j:P * (j + 1)], qz[q][:, p, :, P * j:P * j + w_q],
                                          start=True, stop=True)
                mm.then_inc(sT_ps.sem, 1)

            def score(b, q, n):
                g, i = n // NT, n % NT
                if n == 0:
                    pe.wait_ge(*done(stacks_in, b))
                    pe.wait_ge(*done(s_ok, b - 2))
                    pe.wait_ge(*done(lg_ok, b))
                else:
                    pe.wait_ge(*done(mx_ok, b, n))
                lo = 0 if i else P
                for pr in range(2):
                    o = bank(4 + pr).rearrange("p (r k) -> p r k", r=2)
                    for par in range(2):
                        p = 2 * g + pr
                        nc.tensor.matmul(o[:, par, lo:], qz[q][:, p, par, P * i:P * (i + 1)],
                                         kd[q][:, p, P * (i - 1) + lo:P * (i + 1)], start=par == 0, stop=False,
                                         skip_group_check=True)
                    mm = nc.tensor.matmul(o[:, :, lo:], identb[:], mask[:, :, lo:], start=False, stop=True,
                                          skip_group_check=True)
                mm.then_inc(s_ps.sem, 1)

            def values(b, q, n):
                g, j = n // NT, n % NT
                pe.wait_ge(*done(pt_ok, b, n + 1))
                if n == 0:
                    pe.wait_ge(*done(v_ok, b))
                    pe.wait_ge(*done(h2T_ok, b - 1))
                elif j == 0:
                    pe.wait_ge(*done(ot_ok, b, g))
                w_q = 2 * P if j < NT - 1 else P
                for c in range(HG):
                    mm = nc.tensor.matmul(ps[32 * c:32 * (c + 1), 6, P * j:P * j + w_q], va[:, q, j, HG * g + c, :],
                                          pt[:, n % NPT, c, 0:w_q], start=j == 0, stop=True,
                                          skip_group_check=True)
                mm.then_inc(pv_ps.sem, 1)

            def turn_out(b, g):
                pe.wait_ge(*done(ot_ok, b, g + 1))
                if g == 0:
                    pe.wait_ge(*done(cb_ok, b - 1))
                else:
                    pe.wait_ge(*done(ao_ok, b, g))
                for t in range(NT):
                    mm = nc.tensor.transpose(bank_t(7)[:, t], ot[:, P * t:P * (t + 1)], ident[:])
                mm.then_inc(ott_ps.sem, 1)

            def turn4(k, src):
                for t in range(NT):
                    mm = nc.tensor.transpose(k[:, P * t:P * (t + 1)], src(t), identb[:] if src(t).dtype == BF16 else ident[:])
                return mm

            def body(b, q):
                main, nxt, nx2 = has(b), has(b + 1), has(b + 2)
                for n in range(NCH + 4):
                    if main and n < NCH:
                        score_t(b, q, n)
                    if nxt and n < NCH:
                        score(b + 1, 1 - q, n)
                    if main and 3 <= n < NCH + 3:
                        values(b, q, n - 3)
                    if main and n >= 7 and (n - 7) % NT == 0 and n < NCH + 3:
                        turn_out(b, (n - 7) // NT)
                    if nx2 and n == NCH:
                        pe.wait_ge(*done(h0_ok, b + 2))
                        pe.wait_ge(*done(exp_ok, b, NCH))
                        if not main:
                            pe.wait_ge(*done(hid_ok, b - 1))
                        pe.wait_ge(*done(nfT_ok, b + 1))
                        turn4(bank(0), lambda t: h0[:, t]).then_inc(hT_ps.sem, 1)
                    if nx2 and n == NCH + 2:
                        pe.wait_ge(*done(hT_ok, b + 2))
                        nc.tensor.matmul(bank(1), wq[:], hT[:], start=True, stop=True).then_inc(q_ps.sem, 1)
                        nc.tensor.matmul(bank(2), wk[:], hT[:], start=True, stop=True).then_inc(k_ps.sem, 1)
                if main:
                    turn_out(b, NG - 1)
                if nx2:
                    for t in range(NT):
                        mm = nc.tensor.matmul(bank_t(3)[:, t], hT[:, P * t:P * (t + 1)], wv[:], start=True, stop=True)
                    mm.then_inc(v_ps.sem, 1)
                if nxt:
                    pe.wait_ge(*done(nm_step, b + 1))
                    apart(pe, b)
                    turn = bank_bf(4)[0:NPART * H, :]
                    for t in range(NT):
                        mm = nc.tensor.transpose(turn[:, P * t:P * (t + 1)], nm[:, t].rearrange("p r h -> p (r h)"), identb[:])
                    mm.then_inc(nm_ps.sem, 1)
                    pe.wait_ge(*done(route, b + 1))
                    turn4(bank_bf(5), lambda t: cp[:, t]).then_inc(cT_ps.sem, 1)
                if nx2:
                    for t in range(NT):
                        if t == 0:
                            pe.wait_ge(*done(nmT_ok, b + 1))
                        mm = nc.tensor.matmul(bank_t(4)[:, t], hT[:, P * t:P * (t + 1)], wg[:], start=True, stop=True)
                    mm.then_inc(g_ps.sem, 1)
                if main:
                    pe.wait_ge(*done(ao_ok, b, NG))
                    turn4(bank(7), lambda t: ao[:, t]).then_inc(aoT_ps.sem, 1)
                    pe.wait_ge(*done(st_ok, b))
                    if nxt:
                        pe.wait_ge(*done(cT_ok, b + 1))
                    for t in range(NT):
                        mm = nc.tensor.matmul(bank_t(5)[:, t], st[:, q, P * t:P * (t + 1)], cw[:], start=True, stop=True)
                    mm.then_inc(cw_ps.sem, 1)
                    pe.wait_ge(*done(aoT_ok, b))
                    for t in range(NT):
                        nc.tensor.matmul(bank_t(6)[:, t], aoT[:, P * t:P * (t + 1)], wo[:], start=True, stop=False)
                        mm = nc.tensor.matmul(bank_t(6)[:, t], st[:, q, P * t:P * (t + 1)], ncw[:], start=False, stop=True)
                    mm.then_inc(wo_ps.sem, 1)
                if nx2:
                    nc.tensor.matmul(bank(0), bw[:], hT[:], start=True, stop=True).then_inc(u_ps.sem, 1)

                def up(e):
                    k = 3 * (e % 2)
                    if e < 2 and nx2:
                        for s in ((st_ok, qkr_ok), (v_ok, gpre_ok, s1_ok))[e]:
                            pe.wait_ge(*done(s, b if s is s1_ok else b + 2))
                    elif e == 1:
                        pe.wait_ge(*done(s1_ok, b))
                        if nxt:
                            pe.wait_ge(*done(nmT_ok, b + 1))
                    elif e >= 2:
                        pe.wait_ge(*done(ga_ok, b, e - 1))
                        pe.wait_ge(*done(gc_ok, b, e - 1))
                    for s in range(2):
                        nc.tensor.matmul(bank(k + s), m1[:, e, s], nfT[:, q], start=True, stop=True)
                    nc.tensor.matmul(bank(k + 2), sel[:, e], cT[:, q], start=True, stop=True).then_inc(up_ps.sem, 1)

                def down(e):
                    pe.wait_ge(*done(act_ok, b, e + 1))
                    for t in range(NT):
                        mm = nc.tensor.matmul(bank_t(7)[:, t], act_t[:, e % 2, P * t:P * (t + 1)], m2[:, e], start=False,
                                              stop=e == E - 1, skip_group_check=True)
                    mm.then_inc(down_ps.sem, 1)

                if main:
                    for e in range(E + 1):
                        if e < E:
                            up(e)
                        if e == 0:
                            for t in range(NT):
                                nc.tensor.matmul(bank_t(7)[:, t], cT[:, q, P * t:P * (t + 1)], b2st[:], start=t == 0,
                                                 stop=False, skip_group_check=True)
                        else:
                            down(e - 1)
                        if e == 4:
                            pe.wait_ge(*done(h2_ok, b))
                            pe.wait_ge(*done(t1_ok, b))
                            turn4(bank(6), lambda t: h2[:, t]).then_inc(h2T_ps.sem, 1)
                if nx2:
                    pe.wait_ge(*done(nf_ok, b + 2))
                    if main:
                        pe.wait_ge(*done(gc_ok, b, E))
                    else:
                        pe.wait_ge(*done(qkr_ok, b + 2))
                    turn4(bank_bf(2), lambda t: nf[:, t]).then_inc(nfT_ps.sem, 1)
                    pe.wait_ge(*done(nfT_ok, b + 2))
                    pe.wait_ge(*done(cT_ok, b + 1))
                    for t in range(NT):
                        mm = nc.tensor.matmul(bank(5)[:, E * t:E * (t + 1)], nfT[:, q, P * t:P * (t + 1)], gw[:], start=True, stop=True)
                    mm.then_inc(lg_ps.sem, 1)
                if main:
                    pe.wait_ge(*done(h2T_ok, b))
                    pe.wait_ge(*done(gc_ok, b, E))
                    pe.wait_ge(*done(ga_ok, b, E))
                    for j, k in enumerate((0, 1, 3, 2)):
                        if j == 3:
                            pe.wait_ge(*done(nfT_ok, b + 2)) if nx2 else None
                        nc.tensor.matmul(bank(k), w1[:, P * j:P * (j + 1)], h2T[:], start=True, stop=True).then_inc(w1_ps.sem, 1)
                    for t in range(NT):
                        for j in range(NJ):
                            if t == 0:
                                pe.wait_ge(*done(hid_ok, b, j + 1))
                            mm = nc.tensor.matmul(bank_t(4)[:, t], hid[:, j, P * t:P * (t + 1)], w2[:, j], start=j == 0, stop=j == NJ - 1)
                    mm.then_inc(w2_ps.sem, 1)

            set_spare(pe, "pe_waited")
            schedule(pe, body)

        @block.scalar
        def _(act):
            for k in range(6):
                act.wait_ge(expert_ps.sem, k + 1)
                dst = m1[:, 2 * k:2 * k + 2].rearrange("p e s i -> p (e s i)") if k < 4 else \
                    m2[:, 4 * (k - 4):4 * (k - 3)].rearrange("p e d -> p (e d)")
                nc.scalar.activation(dst, bank_bf(k), ACT.Copy).then_inc(expert_sb.sem, 1)
            all_set(act)

            def body(b, q):
                main, nxt, nx2 = has(b), has(b + 1), has(b + 2)
                if has(b - 1):
                    act.wait_ge(*done(z_ok, b - 1))
                    act.wait_ge(*done(w_ok, b - 2))
                    nc.scalar.activation(zth[:], z[:], ACT.Tanh, scale=0.5).then_inc(zth_ok.sem, 1)
                if nxt:
                    act.wait_ge(*done(gpre_ok, b + 1))
                    act.wait_ge(*done(x1_ok, b - 1))
                    nc.scalar.activation(gth[:, 1 - q], gpre[:], ACT.Tanh, scale=0.5).then_inc(gth_ok.sem, 1)
                for n in range(NCH + 4):
                    if main and n < NCH:
                        act.wait_ge(*done(sT_ps, b, n + 1))
                        if n >= NPT:
                            act.wait_ge(*done(pv_ps, b, n - NPT + 1))
                        else:
                            act.wait_ge(*done(pv_ps, b - 1, NCH - NPT + n + 1))
                        w_q = 2 * P if n % NT < NT - 1 else P
                        src = ps[:, 2 * (n % 2):2 * (n % 2) + 2, :].rearrange("p c (r q) -> p (c r) q", r=2)[:, :, 0:w_q]
                        nc.scalar.activation(pt[:, n % NPT, :, 0:w_q], src, ACT.Exp, scale=SCALE).then_inc(exp_ok.sem, 1)
                    if main and n >= 6 and (n - 6) % NT == 0:
                        g = (n - 6) // NT
                        act.wait_ge(*done(pv_ps, b, NT * (g + 1)))
                        act.wait_ge(*done(ott_ps, b, g))
                        nc.scalar.activation(ot[:], bank(6), ACT.Copy).then_inc(ot_ok.sem, 1)
                    if nxt and n == 5:
                        act.wait_ge(*done(route, b + 1, 4))
                        nc.scalar.activation(ex[:], ld[:], ACT.Exp).then_inc(ex_ok.sem, 1)
                    if nx2 and n == NCH:
                        act.wait_ge(*done(hT_ps, b + 2))
                        act.wait_ge(*done(u_ps, b + 1))
                        nc.scalar.activation(hT[:], bank(0), ACT.Identity, bias=cols["ln1_b"][:], scale=cols["ln1_g"][:]).then_inc(hT_ok.sem, 1)
                if nx2:
                    act.wait_ge(*done(stacks_in, b + 1))
                    for n, (signal_ps, dst, bias) in enumerate(((q_ps, qp, "bQ"), (k_ps, kp, "bK"))):
                        act.wait_ge(*done(signal_ps, b + 2))
                        nc.scalar.activation(dst[:, 0], bank(1 + n), ACT.Identity, bias=cols[bias][:]).then_inc(qkhi_ok.sem, 1)
                if nxt:
                    act.wait_ge(*done(nm_ps, b + 1))
                    act.wait_ge(*done(shift_in, b))
                    nc.scalar.activation(nmT[:], bank_bf(4)[0:NPART * H, :], ACT.Copy).then_inc(nmT_ok.sem, 1)
                    act.wait_ge(*done(cT_ps, b + 1))
                    act.wait_ge(*done(down_ps, b - 1))
                    nc.scalar.activation(cT[:, 1 - q], bank_bf(5), ACT.Copy).then_inc(cT_ok.sem, 1)
                if main:
                    act.wait_ge(*done(aoT_ps, b))
                    act.wait_ge(*done(wo_ps, b - 1))
                    nc.scalar.activation(aoT[:], bank(7), ACT.Copy).then_inc(aoT_ok.sem, 1)
                    for e in range(E):
                        act.wait_ge(*done(up_ps, b, e + 1))
                        if e >= 2:
                            act.wait_ge(*done(gc_ok, b, e - 1))
                        else:
                            act.wait_ge(*done(gc_ok, b - 1))
                        nc.scalar.activation(ga[:, e % 2], bank(3 * (e % 2)), ACT.Gelu_apprx_sigmoid, bias=mbias[:, e, 0:1]).then_inc(ga_ok.sem, 1)
                        if e == 4:
                            act.wait_ge(*done(h2T_ps, b))
                            act.wait_ge(*done(w1_ps, b - 1))
                            nc.scalar.activation(h2T[:], bank(6), ACT.Identity, bias=cols["ln2_b"][:], scale=cols["ln2_g"][:]).then_inc(h2T_ok.sem, 1)
                if nx2:
                    act.wait_ge(*done(nfT_ps, b + 2))
                    nc.scalar.activation(nfT[:, q], bank_bf(2), ACT.Copy).then_inc(nfT_ok.sem, 1)
                if main:
                    for j, k in enumerate((0, 1, 3, 2)):
                        act.wait_ge(*done(w1_ps, b, j + 1))
                        if j == 0:
                            act.wait_ge(*done(w2_ps, b - 1))
                        nc.scalar.activation(hid[:, j], bank(k), ACT.Gelu, bias=b1c[:, j:j + 1]).then_inc(hid_ok.sem, 1)

            schedule(act, body)

        @block.vector
        def _(dve):
            for dst, value in BLANKS:
                nc.vector.memset(dst, value).then_inc(blank_set.sem, 1)
            dve.wait_ge(blank_set.sem, len(BLANKS))
            for dst, value in ONES:
                nc.vector.memset(dst, value).then_inc(blank_set.sem, 1)
            dve.wait_ge(weights_in.sem, 16 * len(WEIGHTS))
            dve.wait_ge(pad_in.sem, 16 * len(PADDED))
            nc.vector.tensor_scalar(ncw[0:N, :], cw[0:N, :], -1.0, None, ALU.mult).then_inc(consts.sem, 1)
            nc.vector.tensor_copy(mbias[:, :, 0:1], mb_b[:, :, 0:1]).then_inc(consts.sem, 1)
            nc.vector.tensor_scalar(mbias[:, :, 1:2], mb_b[:, :, 1:2], 1.0, None, ALU.add).then_inc(consts.sem, 1)
            nc.vector.tensor_copy(gbias[:], gbias_b[:]).then_inc(consts.sem, 1)
            all_set(dve)

            def finish(b):
                dve.wait_ge(*done(zth_ok, b))
                nc.vector.scalar_tensor_tensor(out=zth[:], in0=zth[:], scalar=1.0, in1=z[:], op0=ALU.add, op1=ALU.mult).then_inc(y_ok.sem, 1)
                dve.wait_ge(*done(y_ok, b))
                dve.wait_ge(*done(s_ok, b))
                dve.wait_ge(*done(ob_ok, b - 1))
                nc.vector.scalar_tensor_tensor(out=w[:], in0=zth[:], scalar=0.5, in1=sres[:], op0=ALU.mult, op1=ALU.mult).then_inc(w_ok.sem, 1)

            def norm_stats(b, q):
                dve.wait_ge(*done(x_in, b))
                dve.wait_ge(*done(mv_ok, b - 1))
                for t in range(NT):
                    bn = nc.vector.bn_stats(stats[:, t], xl[:, q, t])
                bn.then_inc(stats_ok.sem, 1)
                dve.wait_ge(*done(stats_ok, b))
                dve.wait_ge(*done(xn_ok, b - 1))
                apart(dve, b)
                for t in range(NT):
                    bn = nc.vector.bn_aggr(mv[:, t], stats[:, t])
                bn.then_inc(mv_ok.sem, 1)

            def norm_x(b, q):
                dve.wait_ge(*done(r1_step, b))
                dve.wait_ge(*done(xn_copied, b - 2))
                for t in range(NT):
                    ts = nc.vector.tensor_scalar(xn[:, q, t], xl[:, q, t], mv[:, t, 0:1], r1[:, t:t + 1], ALU.subtract, ALU.mult)
                ts.then_inc(xn_ok.sem, 1)

            def squares(b, q):
                dve.wait_ge(*done(xn_ok, b))
                dve.wait_ge(*done(xc_copied, b - 2))
                nc.vector.tensor_copy(xc[:, q], xn[:, q]).then_inc(xc_ok.sem, 1)
                dve.wait_ge(*done(xc_ok, b))
                dve.wait_ge(*done(rs_step, b - 1))
                for t in range(NT):
                    tr = nc.vector.tensor_tensor_reduce(junk[:, t], xc[:, q, t], xc[:, q, t], 1.0, 0.0, ALU.mult, ALU.add, sq[:, t:t + 1])
                tr.then_inc(sq_ok.sem, 1)

            def norm_h(b, q):
                dve.wait_ge(*done(r2_step, b))
                dve.wait_ge(*done(hT_ps, b - 1))
                for t in range(NT):
                    ts = nc.vector.tensor_scalar(h0[:, t], xn[:, q, t], r2[:, t:t + 1], None, ALU.mult)
                ts.then_inc(h0_ok.sem, 1)

            def norm_f(b, q):
                dve.wait_ge(*done(rs_step, b))
                dve.wait_ge(*done(nfT_ps, b - 1))
                for t in range(NT):
                    ts = nc.vector.scalar_tensor_tensor(out=nf[:, t], in0=xc[:, q, t], scalar=rs[:, t:t + 1], in1=rows["nw"][:],
                                                        op0=ALU.mult, op1=ALU.mult)
                ts.then_inc(nf_ok.sem, 1)

            def route_rank(b):
                dve.wait_ge(*done(lg_ok, b))
                shape = [P, NT, E, E]
                nc.vector.tensor_tensor(dl[:], lg[:].unsqueeze(2).to_broadcast(shape), lg[:].unsqueeze(3).to_broadcast(shape),
                                        ALU.subtract).then_inc(route.sem, 1)
                nc.vector.tensor_reduce(lmax[:], lg[:], AX.X, ALU.max).then_inc(route.sem, 1)
                dve.wait_ge(*done(route, b, 2))
                nc.vector.tensor_tensor(bt[:], dl[:], tie[:].unsqueeze(1).to_broadcast(shape), ALU.is_gt).then_inc(route.sem, 1)
                nc.vector.tensor_tensor(ld[:], lg[:], lmax[:].unsqueeze(2).to_broadcast([P, NT, E]), ALU.subtract).then_inc(route.sem, 1)
                dve.wait_ge(*done(route, b, 4))
                nc.vector.tensor_reduce(rank[:], bt[:], AX.X, ALU.add).then_inc(route.sem, 1)

            def route_mix(b):
                dve.wait_ge(*done(route, b, 5))
                dve.wait_ge(*done(ex_ok, b))
                nc.vector.scalar_tensor_tensor(out=exs[:], in0=rank[:], scalar=2.0, in1=ex[:], op0=ALU.is_lt, op1=ALU.mult).then_inc(route.sem, 1)
                dve.wait_ge(*done(route, b, 6))
                nc.vector.tensor_reduce(zs[:], exs[:], AX.X, ALU.add).then_inc(route.sem, 1)
                dve.wait_ge(*done(route, b, 7))
                nc.vector.reciprocal(zr[:], zs[:]).then_inc(route.sem, 1)
                dve.wait_ge(*done(route, b, 8))
                nc.vector.tensor_tensor(cmb[:], exs[:], zr[:].unsqueeze(2).to_broadcast([P, NT, E]), ALU.mult).then_inc(route.sem, 1)
                dve.wait_ge(*done(route, b, 9))
                dve.wait_ge(*done(cT_ps, b - 1))
                nc.vector.tensor_copy(cp[:, :, 0:E], cmb[:]).then_inc(route.sem, 1)
                dve.wait_ge(*done(route, b, 10))
                nc.vector.tensor_tensor(cr[:], cmb[:], cp[:, :, 0:E], ALU.subtract).then_inc(route.sem, 1)
                dve.wait_ge(*done(route, b, 11))
                nc.vector.tensor_copy(cp[:, :, E:2 * E], cr[:]).then_inc(cpm.sem, 1)
                dve.wait_ge(*done(cpm, b))
                nc.vector.tensor_tensor(cp[:, :, 2 * E:3 * E], cr[:], cp[:, :, E:2 * E], ALU.subtract).then_inc(route.sem, 1)

            cpm = signal("cpm", 1)

            def body(b, q):
                main, nxt, nx2 = has(b), has(b + 1), has(b + 2)
                for n in range(NCH + 5):
                    if nxt and n < NCH:
                        g, i = n // NT, n % NT
                        dve.wait_ge(*done(s_ps, b + 1, n + 1))
                        if n == 0:
                            dve.wait_ge(*done(nm_step, b))
                        lo = 0 if i else P
                        src = ps[:, 4:6, :].rearrange("p c (r k) -> p (c r) k", r=2)[:, :, lo:]
                        nc.vector.tensor_reduce(mx[:, i, HG * g:HG * (g + 1)], src, AX.X, ALU.max).then_inc(mx_ok.sem, 1)
                    if n == 0 and has(b - 1):
                        finish(b - 1)
                    if nx2:
                        if n == 3:
                            norm_stats(b + 2, q)
                        if n == 6:
                            norm_x(b + 2, q)
                        if n == 7:
                            squares(b + 2, q)
                        if n == 10:
                            norm_h(b + 2, q)
                        if n == 13:
                            norm_f(b + 2, q)
                    if nxt and n == 2:
                        route_rank(b + 1)
                    if nxt and n == 8:
                        route_mix(b + 1)
                    if nxt and n == NCH:
                        dve.wait_ge(*done(mx_ok, b + 1))
                        dve.wait_ge(*done(nm_ps, b))
                        nc.vector.tensor_scalar(nm[:, :, 0], mx[:], -1.0, None, ALU.mult).then_inc(nm_step.sem, 1)
                        dve.wait_ge(*done(nm_step, b + 1, 1))
                        nc.vector.scalar_tensor_tensor(out=mr[:], in0=mx[:], scalar=-1.0, in1=nm[:, :, 0], op0=ALU.mult, op1=ALU.subtract).then_inc(nm_step.sem, 1)
                        dve.wait_ge(*done(nm_step, b + 1, 2))
                        nc.vector.tensor_copy(nm[:, :, 1], mr[:]).then_inc(nm_step.sem, 1)
                        dve.wait_ge(*done(nm_step, b + 1, 3))
                        nc.vector.tensor_tensor(nm[:, :, 2], mr[:], nm[:, :, 1], ALU.subtract).then_inc(nm_step.sem, 1)
                    if main and n >= 8 and (n - 8) % NT == 0:
                        g = (n - 8) // NT
                        dve.wait_ge(*done(ott_ps, b, g + 1))
                        if g == 0:
                            dve.wait_ge(*done(aoT_ps, b - 1))
                        o = bank_t(7).rearrange("p t (h v) -> p t h v", v=VW)
                        dve.wait_ge(*done(ao_ok, b, g))
                        nc.vector.reciprocal(rz[:], o[:, :, :, DH]).then_inc(rz_ok.sem, 1)
                        dve.wait_ge(*done(rz_ok, b, g + 1))
                        nc.vector.tensor_tensor(ao[:, :, HG * DH * g:HG * DH * (g + 1)].rearrange("p t (h v) -> p t h v", v=DH),
                                                o[:, :, :, 0:DH], rz[:].unsqueeze(3).to_broadcast([P, NT, HG, DH]), ALU.mult).then_inc(ao_ok.sem, 1)
                if nx2:
                    for n, (hi, rest, bias) in enumerate(((qp, qr, "bQ"), (kp, kr, "bK"))):
                        dve.wait_ge(*done(qkhi_ok, b + 2, n + 1))
                        dve.wait_ge(*done(qklo_ok, b + 1, n + 1))
                        nc.vector.scalar_tensor_tensor(out=rest[:], in0=bank(1 + n), scalar=cols[bias][:], in1=hi[:, 0],
                                                       op0=ALU.add, op1=ALU.subtract).then_inc(qkr_ok.sem, 1)
                    dve.wait_ge(*done(v_ps, b + 2))
                    dve.wait_ge(*done(pv_ps, b))
                    shape = [P, NT, H, DH]
                    nc.vector.tensor_tensor(va[:, q, :, :, 0:DH], bank_t(3).rearrange("p t (h v) -> p t h v", v=DH),
                                            rows["bV"][:].rearrange("p (h v) -> p h v", v=DH).unsqueeze(1).to_broadcast(shape), ALU.add).then_inc(v_ok.sem, 1)
                    dve.wait_ge(*done(g_ps, b + 2))
                    dve.wait_ge(*done(gth_ok, b + 1))
                    nc.vector.tensor_tensor(gpre[:], bank_t(4), rows["bg"][:].unsqueeze(1).to_broadcast([P, NT, D]), ALU.add).then_inc(gpre_ok.sem, 1)
                if main:
                    dve.wait_ge(*done(cw_ps, b))
                    dve.wait_ge(*done(xn_copied, b))
                    nc.vector.tensor_tensor(s1[:], bank_t(5), xnr[:], ALU.add).then_inc(s1_ok.sem, 1)
                    dve.wait_ge(*done(wo_ps, b))
                    dve.wait_ge(*done(gth_ok, b))
                    nc.vector.scalar_tensor_tensor(out=t1[:], in0=gth[:, q], scalar=1.0, in1=bank_t(6), op0=ALU.add, op1=ALU.mult).then_inc(t1_ok.sem, 1)
                    dve.wait_ge(*done(t1_ok, b))
                    dve.wait_ge(*done(s1_ok, b))
                    dve.wait_ge(*done(x1b_ok, b - 1))
                    nc.vector.scalar_tensor_tensor(out=x1[:], in0=t1[:], scalar=0.5, in1=s1[:], op0=ALU.mult, op1=ALU.add).then_inc(x1_ok.sem, 1)
                if nx2:
                    dve.wait_ge(*done(u_ps, b + 2))
                    dve.wait_ge(*done(wo_ps, b))
                    nc.vector.tensor_tensor_scan(st[0:N, q], acol[0:N, :].to_broadcast([N, T]), bank(0)[0:N], 0.0, ALU.mult, ALU.add).then_inc(st_ok.sem, 1)
                if main:
                    dve.wait_ge(*done(x1_ok, b))
                    for t in range(NT):
                        bn = nc.vector.bn_stats(st2[:, t], x1[:, t])
                    bn.then_inc(st2_ok.sem, 1)
                    dve.wait_ge(*done(st2_ok, b))
                    apart(dve, b)
                    for t in range(NT):
                        bn = nc.vector.bn_aggr(mv2[:, t], st2[:, t])
                    bn.then_inc(mv2_ok.sem, 1)
                    for e in range(E):
                        k = 3 * (e % 2)
                        dve.wait_ge(*done(up_ps, b, e + 1))
                        if e >= 2:
                            dve.wait_ge(*done(act_ok, b, e - 1))
                        nc.vector.tensor_scalar(lin[:, e % 2], bank(k + 1), mbias[:, e, 1:2], 1.0 - LIMIT, ALU.add, ALU.max).then_inc(lin_ok.sem, 1)
                        dve.wait_ge(*done(ga_ok, b, e + 1))
                        nc.vector.scalar_tensor_tensor(out=gc[:, e % 2], in0=ga[:, e % 2], scalar=G_LIMIT, in1=bank(k + 2),
                                                       op0=ALU.min, op1=ALU.mult).then_inc(gc_ok.sem, 1)
                        dve.wait_ge(*done(gc_ok, b, e + 1))
                        if e >= 2:
                            dve.wait_ge(*done(down_ps, b, e - 1))
                        else:
                            dve.wait_ge(*done(down_ps, b - 1))
                        nc.vector.scalar_tensor_tensor(out=act_t[:, e % 2], in0=lin[:, e % 2], scalar=1.0 + LIMIT, in1=gc[:, e % 2],
                                                       op0=ALU.min, op1=ALU.mult).then_inc(act_ok.sem, 1)
                        if e == 2:
                            dve.wait_ge(*done(r3_step, b))
                            dve.wait_ge(*done(h2T_ps, b - 1))
                            for t in range(NT):
                                ts = nc.vector.tensor_scalar(h2[:, t], x1[:, t], mv2[:, t, 0:1], r3[:, t:t + 1], ALU.subtract, ALU.mult)
                            ts.then_inc(h2_ok.sem, 1)
                if main:
                    dve.wait_ge(*done(down_ps, b))
                    nc.vector.tensor_copy(cb[:], bank_t(7)).then_inc(cb_ok.sem, 1)
                    dve.wait_ge(*done(cb_ok, b))
                    dve.wait_ge(*done(xc_copied, b))
                    nc.vector.tensor_tensor(z[:], xcr[:], cb[:], ALU.add).then_inc(z_ok.sem, 1)
                if nx2:
                    dve.wait_ge(*done(lg_ps, b + 2))
                    dve.wait_ge(*done(route, b + 1))
                    nc.vector.tensor_tensor(lg[:], bank(5)[:, 0:NT * E].rearrange("p (t e) -> p t e", e=E),
                                            gbias[:].unsqueeze(1).to_broadcast([P, NT, E]), ALU.add).then_inc(lg_ok.sem, 1)
                if main:
                    dve.wait_ge(*done(w2_ps, b))
                    dve.wait_ge(*done(x1b_ok, b))
                    nc.vector.tensor_tensor(sres[:], bank_t(4), x1b[:], ALU.add).then_inc(s_ok.sem, 1)

            set_spare(dve, "dve_waited")
            schedule(dve, body)

        @block.gpsimd
        def _(pool):
            pool.wait_ge(blank_set.sem, len(BLANKS))
            sg = lambda i: i.then_inc(pool_set.sem, 1)
            for m in (ident, identb):
                sg(nc.gpsimd.affine_select(out=m[:], in_=m[:], compare_op=ALU.not_equal, fill=1.0, base=0, pattern=[[-1, P]], channel_multiplier=1))
            sg(nc.gpsimd.affine_select(out=mask[:, :, 0:P], in_=mask[:, :, 0:P], compare_op=ALU.is_ge, fill=NEG, base=-1, pattern=[[0, 2], [1, P]], channel_multiplier=-1))
            sg(nc.gpsimd.affine_select(out=mask[:, :, P:], in_=mask[:, :, P:], compare_op=ALU.is_ge, fill=NEG, base=0, pattern=[[0, 2], [-1, P]], channel_multiplier=1))
            sg(nc.gpsimd.affine_select(out=tie[:], in_=tie[:], compare_op=ALU.is_ge, fill=TIE, base=0, pattern=[[-1, E], [1, E]], channel_multiplier=0))
            for c in range(NPART):
                if c:
                    pool.wait_ge(pool_set.sem, 5 + c)
                sg(nc.gpsimd.affine_select(out=sel[:], in_=sel[:], compare_op=ALU.not_equal, fill=1.0, base=-E * c, pattern=[[-1, E], [0, P]], channel_multiplier=1))
            sg(nc.gpsimd.tensor_copy(vt[:], half[:]))
            all_set(pool)

            def inv_root(dst, tmp, src, scale, step, b, first, free):
                for s, sb_, c in free:
                    pool.wait_ge(*done(s, sb_, c))
                apart(pool, b)
                nc.gpsimd.tensor_scalar(tmp, src, scale, EPS, ALU.mult, ALU.add).then_inc(step.sem, 1)
                pool.wait_ge(*done(step, b, first + 1))
                nc.gpsimd.tensor_tensor(dst, tmp, half[:], ALU.pow).then_inc(step.sem, 1)

            def body(b, q):
                main, nxt, nx2 = has(b), has(b + 1), has(b + 2)
                for n in range(NCH + 1):
                    if main and n < NCH:
                        s = n % NPT
                        pool.wait_ge(*done(exp_ok, b, n + 1))
                        apart(pool, b)
                        sel1 = nc.gpsimd.affine_select(out=pt[:, s, :, 0:P], in_=pt[:, s, :, 0:P], compare_op=ALU.is_ge, fill=0.0, base=0,
                                                       pattern=[[0, HG], [1, P]], channel_multiplier=-1)
                        if n % NT < NT - 1:
                            sel1 = nc.gpsimd.affine_select(out=pt[:, s, :, P:], in_=pt[:, s, :, P:], compare_op=ALU.is_ge, fill=0.0, base=-1,
                                                           pattern=[[0, HG], [-1, P]], channel_multiplier=1)
                        sel1.then_inc(pt_ok.sem, 1)
                    if n == 1 and has(b - 1):
                        pool.wait_ge(*done(w_ok, b - 1))
                        pool.wait_ge(*done(xr_in, b - 1))
                        pool.wait_ge(*done(out_st, b - 2))
                        nc.gpsimd.tensor_tensor(ob[:], w[:], xr[:], ALU.add).then_inc(ob_ok.sem, 1)
                    if nx2 and n == 4:
                        pool.wait_ge(*done(mv_ok, b + 2))
                        inv_root(r1[:], r1t[:], mv[:, :, 1], 1.0, r1_step, b + 2, 0, ((xn_ok, b + 1, None),))
                    if nx2 and n == 6:
                        pool.wait_ge(*done(r1_step, b + 2))
                        nc.gpsimd.tensor_tensor(vv[:], mv[:, :, 1], r1[:], ALU.mult).then_inc(r2_step.sem, 1)
                        pool.wait_ge(*done(r2_step, b + 2, 1))
                        nc.gpsimd.tensor_tensor(vt[:], vv[:], r1[:], ALU.mult).then_inc(r2_step.sem, 1)
                        pool.wait_ge(*done(r2_step, b + 2, 2))
                        inv_root(r2[:], v2t[:], vt[:], 1.0, r2_step, b + 2, 2, ((h0_ok, b + 1, None),))
                    if nx2 and n == 9:
                        pool.wait_ge(*done(sq_ok, b + 2))
                        inv_root(rs[:], sqm[:], sq[:], 1.0 / D, rs_step, b + 2, 0, ((nf_ok, b + 1, None),))
                if nx2:
                    for n, (parts, rest) in enumerate(((qp, qr), (kp, kr))):
                        pool.wait_ge(*done(qkr_ok, b + 2, n + 1))
                        apart(pool, b)
                        nc.gpsimd.tensor_copy(parts[:, 1], rest[:]).then_inc(qkmid_ok.sem, 1)
                        pool.wait_ge(*done(qkmid_ok, b + 2, n + 1))
                        nc.gpsimd.tensor_tensor(parts[:, 2], rest[:], parts[:, 1], ALU.subtract).then_inc(qklo_ok.sem, 1)
                if main:
                    pool.wait_ge(*done(mv2_ok, b))
                    inv_root(r3[:], r3t[:], mv2[:, :, 1], 1.0, r3_step, b, 0, ((h2_ok, b - 1, None),))
                    pool.wait_ge(*done(x1_ok, b))
                    pool.wait_ge(*done(s_ok, b - 1))
                    nc.gpsimd.tensor_tensor(x1b[:], x1[:], rows["b2"][:].unsqueeze(1).to_broadcast([P, NT, D]), ALU.add).then_inc(x1b_ok.sem, 1)

            r3t = sb("r3t", [P, NT])
            set_spare(pool, "pool_waited")
            schedule(pool, body)


_NAMES = {
    "x": "L0_attn_x", "ln1_g": "L0_attn_ln1_g", "ln1_b": "L0_attn_ln1_b", "WQ": "L0_attn_WQ", "bQ": "L0_attn_bQ",
    "WK": "L0_attn_WK", "bK": "L0_attn_bK", "WV": "L0_attn_WV", "bV": "L0_attn_bV", "WO": "L0_attn_WO",
    "bO": "L0_attn_bO", "Wg": "L0_attn_Wg", "bg": "L0_attn_bg", "A": "L0_attn_A", "Bw": "L0_attn_Bw",
    "Cw": "L0_attn_Cw", "ln2_g": "L0_attn_ln2_g", "ln2_b": "L0_attn_ln2_b", "W1": "L0_attn_W1", "b1": "L0_attn_b1",
    "W2": "L0_attn_W2", "b2": "L0_attn_b2", "norm_weight": "L0_ffn_norm_weight", "gate_weight": "L0_ffn_gate_weight",
    "gate_bias": "L0_ffn_gate_bias", "mlp1_weight": "L0_ffn_mlp1_weight", "mlp1_bias": "L0_ffn_mlp1_bias",
    "mlp2_weight": "L0_ffn_mlp2_weight", "mlp2_bias": "L0_ffn_mlp2_bias",
}


def kernel(**inputs):
    import concourse.bacc as bacc
    from concourse.bass_utils import run_bass_kernel_spmd as run

    nc = bacc.Bacc("TRN2", target_bir_lowering=False, num_devices=1)
    arrays, args = {}, {}
    for short, name in _NAMES.items():
        v = np.ascontiguousarray(inputs[name])
        arrays[name] = v
        args[short] = nc.dram_tensor(name, v.shape, mybir.dt.from_np(v.dtype), kind="ExternalInput").ap()
    out = nc.dram_tensor("out", (B, T, D), F32, kind="ExternalOutput").ap()
    build(nc, args, out)
    return run(nc, [arrays], core_ids=[0]).results[0]["out"]
```

```python
from contextlib import ExitStack

import numpy as np

import concourse.bass as bass
from concourse import mybir

ALU = mybir.AluOpType
ACT = mybir.ActivationFunctionType
AX = mybir.AxisListType
F32 = mybir.dt.float32
BF16 = mybir.dt.bfloat16

B, T, D = 16, 512, 128
P = 128
NT = T // P
H, DH = 16, 8
NPAIR = H // 2
HG = 4
NG = H // HG
NCH = NG * NT
N = 64
DFF = 512
NJ = DFF // P
E, I = 8, 128
VW = 32
NPART = 3
SHIFT = 6 * DH
EPS = 1e-5
LIMIT, ALPHA = 7.0, 1.702
G_LIMIT = float(LIMIT / (1.0 + np.exp(-ALPHA * LIMIT)))
SCALE = float(1.0 / np.sqrt(np.float32(DH)))
NEG = -1e30
TIE = -1e-37
CONSTS = 4


class Signal:

    def __init__(self, sem, per):
        self.sem, self.per = sem, per


def build(nc, a, out):
    with ExitStack() as ctx:
        def sb(name, shape, dt=F32):
            return ctx.enter_context(nc.sbuf_tensor(name, shape, dt))

        def signal(name, per):
            return Signal(ctx.enter_context(nc.semaphore(name)), per)

        ps = ctx.enter_context(nc.psum_tensor("ps", [P, 8, 512], F32))

        def bank(k):
            return ps[:, k, :]

        def bank_t(k):
            return ps[:, k, :].rearrange("p (t d) -> p t d", t=NT)

        def bank_bf2(k):
            return ps[:, k, :].bitcast(BF16)[:, T:]

        def bank_bf(k):
            return ps[:, k, :].bitcast(BF16)[:, 0:T]

        ident = sb("ident", [P, P])
        identb = sb("identb", [P, P], BF16)
        mask = sb("mask", [P, 2, 2 * P], BF16)
        sel = sb("sel", [P, E, P], BF16)
        tie = sb("tie", [P, E, E])
        half = sb("half", [P, NT])
        zrow = sb("zrow", [NPART, T], BF16)
        wq, wk, wv, wo, wg = (sb(n, [P, P]) for n in ("wq", "wk", "wv", "wo", "wg"))
        bw = sb("bw", [P, P])
        cw = sb("cw", [P, P])
        ncw = sb("ncw", [P, P])
        w1 = sb("w1", [P, DFF])
        w2 = sb("w2", [P, NJ, P])
        cols = {n: sb(n, [P, 1]) for n in ("ln1_g", "ln1_b", "bQ", "bK", "ln2_g", "ln2_b")}
        b1c = sb("b1c", [P, NJ])
        acol = sb("acol", [P, 1])
        rows = {n: sb("row_" + n, [P, P]) for n in ("bV", "bg", "b2", "nw")}
        gbias_b = sb("gbias_b", [P, E], BF16)
        gbias = sb("gbias", [P, E])
        gw = sb("gw", [P, E], BF16)
        m1 = sb("m1", [P, E, 2, P], BF16)
        m2 = sb("m2", [P, E, P])
        mb_b = sb("mb_b", [P, E, 2], BF16)
        mbias = sb("mbias", [P, E, 2])
        b2st = sb("b2st", [P, P], BF16)

        xl = sb("xl", [P, 2, NT, D])
        stats = sb("stats", [P, NT, 6])
        mv = sb("mv", [P, NT, 2])
        r1, r1t, vv, r2, sq, sqm, rs = (sb(n, [P, NT]) for n in ("r1", "r1t", "vv", "r2", "sq", "sqm", "rs"))
        vt = sb("vt", [P, NT])
        xn = sb("xn", [P, 2, NT, D])
        xc = sb("xc", [P, 2, NT, D], BF16)
        junk = sb("junk", [P, NT, D], BF16)
        h0 = sb("h0", [P, NT, D])
        nf = sb("nf", [P, NT, D], BF16)
        hT = sb("hT", [P, T])
        nfT = sb("nfT", [P, 2, T], BF16)
        nfn = sb("nfn", [P, T], BF16)
        qp = sb("qp", [P, NPART, T], BF16)
        kp = sb("kp", [P, NPART, T], BF16)
        qr = sb("qr", [P, T])
        kr = sb("kr", [P, T])
        qz = [sb(f"qz{i}", [P, NPAIR, 2, T], BF16) for i in range(2)]
        kd = [sb(f"kd{i}", [P, NPAIR, T], BF16) for i in range(2)]
        va = sb("va", [P, 2, NT, H, VW])
        st = sb("st", [P, 2, T])
        gpre = sb("gpre", [P, NT, D])
        gth = sb("gth", [P, 2, NT, D])
        mx = sb("mx", [P, NT, H])
        mr = sb("mr", [P, NT, H])
        nm = sb("nm", [P, NT, NPART, H], BF16)
        nmT = sb("nmT", [NPART * H, T], BF16)
        NPT = 4
        pt = sb("pt", [P, NPT, HG, 2 * P])
        m1raw = pt[:, 0].rearrange("p h q -> p (h q)").bitcast(BF16).rearrange("p (e s h) -> p e s h", e=E, s=2)
        m2raw = pt[:, 1].rearrange("p h q -> p (h q)").bitcast(BF16)[:, 0:E * P].rearrange("p (e i) -> p e i", e=E)
        ot = sb("ot", [P, T])
        rz = sb("rz", [P, NT, HG])
        ao = sb("ao", [P, NT, H * DH])
        aoT = sb("aoT", [P, T])
        lg = sb("lg", [P, NT, E], BF16)
        dl = sb("dl", [P, NT, E, E])
        bt = sb("bt", [P, NT, E, E])
        rank = sb("rank", [P, NT, E])
        lmax = sb("lmax", [P, NT])
        ld = sb("ld", [P, NT, E])
        ex = sb("ex", [P, NT, E])
        exs = sb("exs", [P, NT, E])
        zs = sb("zs", [P, NT])
        zr = sb("zr", [P, NT])
        cmb = sb("cmb", [P, NT, E])
        cr = sb("cr", [P, NT, E])
        cp = sb("cp", [P, NT, P], BF16)
        cT = sb("cT", [P, 2, T], BF16)
        xnr = sb("xnr", [P, NT, D])
        xcr = sb("xcr", [P, NT, D], BF16)
        xr = sb("xr", [P, NT, D])
        s1 = sb("s1", [P, NT, D])
        x1 = sb("x1", [P, NT, D])
        x1b = sb("x1b", [P, NT, D])
        st2 = sb("st2", [P, NT, 6])
        mv2 = sb("mv2", [P, NT, 2])
        v2t = sb("v2t", [P, NT])
        r3 = sb("r3", [P, NT])
        h2 = sb("h2", [P, NT, D])
        h2T = sb("h2T", [P, T])
        hid = sb("hid", [P, NJ, T])
        sres = sb("sres", [P, NT, D])
        ga = sb("ga", [P, 2, T])
        lin = sb("lin", [P, 2, T])
        gc = sb("gc", [P, 2, T])
        act_t = sb("act_t", [P, 3, T])
        cb = sb("cb", [P, NT, D], BF16)
        z = sb("z", [P, NT, D], BF16)
        zth = sb("zth", [P, NT, D])
        ob = sb("ob", [P, NT, D])

        blank_set = signal("blank_set", 1)
        pool_set = signal("pool_set", 1)
        weights_in = signal("weights_in", 1)
        pad_in = signal("pad_in", 1)
        expert_ps = signal("expert_ps", 1)
        expert_sb = signal("expert_sb", 1)
        consts = signal("consts", 1)
        x_in = signal("x_in", 16)
        xr_in = signal("xr_in", 16)
        xn_copied = signal("xn_copied", 16)
        xc_copied = signal("xc_copied", 16)
        stacks_in = signal("stacks_in", 16 * 6)
        qk_out = signal("qk_out", 16 * 6)
        nm_out = signal("nm_out", 16)
        shift_in = signal("shift_in", 16 * 2)
        out_st = signal("out_st", 16)
        stats_ok = signal("stats_ok", 2)
        mv_ok = signal("mv_ok", 1)
        r1_step = signal("r1_step", 2)
        r2_step = signal("r2_step", 4)
        xn_ok = signal("xn_ok", 2)
        xc_ok = signal("xc_ok", 1)
        sq_ok = signal("sq_ok", 2)
        rs_step = signal("rs_step", 2)
        h0_ok = signal("h0_ok", NT)
        nf_ok = signal("nf_ok", 2)
        hT_ps = signal("hT_ps", 1)
        hT_ok = signal("hT_ok", 1)
        q_ps = signal("q_ps", 1)
        k_ps = signal("k_ps", 1)
        v_ps = signal("v_ps", 1)
        u_ps = signal("u_ps", 1)
        g_ps = signal("g_ps", 1)
        qkhi_ok = signal("qkhi_ok", 2)
        qkr_ok = signal("qkr_ok", 2)
        qkmid_ok = signal("qkmid_ok", 2)
        qklo_ok = signal("qklo_ok", 2)
        v_ok = signal("v_ok", 1)
        st_ok = signal("st_ok", 1)
        gpre_ok = signal("gpre_ok", 1)
        gth_ok = signal("gth_ok", 1)
        s_ps = signal("s_ps", 2 * NCH)
        mx_ok = signal("mx_ok", 2 * NCH)
        nm_step = signal("nm_step", 4)
        nm_ps = signal("nm_ps", 1)
        nmT_ok = signal("nmT_ok", 1)
        sT_ps = signal("sT_ps", NCH)
        exp_ok = signal("exp_ok", NCH)
        pt_ok = signal("pt_ok", NCH)
        pv_ps = signal("pv_ps", NCH)
        ot_ok = signal("ot_ok", NG)
        ott_ps = signal("ott_ps", NG)
        rz_ok = signal("rz_ok", NG)
        ao_ok = signal("ao_ok", NG)
        aoT_ps = signal("aoT_ps", 1)
        aoT_ok = signal("aoT_ok", 1)
        wo_ps = signal("wo_ps", 1)
        cw_ps = signal("cw_ps", 1)
        t1_ok = signal("t1_ok", 1)
        s1_ok = signal("s1_ok", 1)
        x1_ok = signal("x1_ok", 1)
        x1b_ok = signal("x1b_ok", 1)
        st2_ok = signal("st2_ok", 1)
        mv2_ok = signal("mv2_ok", 1)
        r3_step = signal("r3_step", 2)
        h2_ok = signal("h2_ok", 1)
        h2T_ps = signal("h2T_ps", 1)
        h2T_ok = signal("h2T_ok", 1)
        w1_ps = signal("w1_ps", NJ)
        hid_ok = signal("hid_ok", NJ)
        w2_ps = signal("w2_ps", 1)
        s_ok = signal("s_ok", 1)
        nfT_ps = signal("nfT_ps", 1)
        nfn_ok = signal("nfn_ok", 1)
        nfT_ok = signal("nfT_ok", 1)
        lg_ps = signal("lg_ps", 1)
        lg_ok = signal("lg_ok", 1)
        route = signal("route", 13)
        ex_ok = signal("ex_ok", 1)
        cT_ps = signal("cT_ps", 1)
        cT_ok = signal("cT_ok", 1)
        up_ps = signal("up_ps", E)
        ga_ok = signal("ga_ok", E)
        lin_ok = signal("lin_ok", E)
        clip_ok = signal("clip_ok", E)
        gc_ok = signal("gc_ok", E)
        act_ok = signal("act_ok", E)
        down_ps = signal("down_ps", E)
        cb_ok = signal("cb_ok", 1)
        z_ok = signal("z_ok", 1)
        zth_ok = signal("zth_ok", 1)
        y_ok = signal("y_ok", 1)
        w_ok = signal("w_ok", 1)
        ob_ok = signal("ob_ok", 1)

        spare = {}

        def apart(eng, b):
            if not isinstance(b, int):
                eng.sem_inc(spare[eng], 1)

        def set_spare(eng, name):
            spare[eng] = ctx.enter_context(nc.semaphore(name))

        def done(signal, batch, count=None):
            value = batch * signal.per + (signal.per if count is None else count)
            if isinstance(value, int) and value <= 0:
                return consts.sem, CONSTS
            return signal.sem, value

        x_d = a["x"].rearrange("b (t p) d -> b p t d", p=P)
        o_d = out.rearrange("b (t p) d -> b p t d", p=P)

        def row_of(v):
            return v.rearrange("(o d) -> o d", o=1).broadcast_to([P, v.shape[0]])

        def col_of(v, n=1):
            return v.rearrange("(j p) -> p j", j=n)

        WEIGHTS = [
            (wq[:], a["WQ"]), (wk[:], a["WK"]), (wv[:], a["WV"]), (wo[:], a["WO"]), (wg[:], a["Wg"]),
            (w1[:], a["W1"]), (w2[:], a["W2"].rearrange("(j p) d -> p j d", j=NJ)),
            *((cols[n][:], col_of(a[n])) for n in cols),
            (b1c[:], col_of(a["b1"], NJ)), (acol[0:N, :], col_of(a["A"])),
            (rows["bV"][:], row_of(a["bV"])), (rows["bg"][:], row_of(a["bg"])),
            (rows["b2"][:], row_of(a["b2"])), (rows["nw"][:], row_of(a["norm_weight"])),
            (gbias_b[:], row_of(a["gate_bias"])), (gw[:], a["gate_weight"].rearrange("e h -> h e")),
            (m1raw[:], a["mlp1_weight"].rearrange("e (i s) h -> i e s h", s=2)),
            (m2raw[:], a["mlp2_weight"].rearrange("e h i -> h e i")),
            (mb_b[:], a["mlp1_bias"].rearrange("e (i s) -> i e s", s=2)),
        ]
        PADDED = [
            (bw[:, 0:N], a["Bw"]), (cw[0:N, :], a["Cw"]),
            (ncw[N:N + 1, :], a["bO"].rearrange("(o d) -> o d", o=1)),
            *((b2st[E * c:E * (c + 1), :], a["mlp2_bias"]) for c in range(NPART)),
        ]
        BLANKS = [
            (mask[:], 0.0), (sel[:], 0.0), (tie[:], 0.0), (half[:], -0.5), (zrow[:], 0.0),
            (ident[:], 0.0), (identb[:], 0.0), (bw[:], 0.0), (cw[:], 0.0), (ncw[:], 0.0), (b2st[:], 0.0),
            (st[:], 0.0), (va[:], 0.0), (cp[:], 0.0), *((q[:], 0.0) for q in qz),
        ]
        ONES = [
            *((k[32 * r:32 * (r + 1)], 1.0) for k in kd for r in (1, 3)),
            (st[N:N + 1], 1.0), *((va[:, i, :, :, DH:DH + 1], 1.0) for i in range(2)),
        ]

        qk_d = nc.dram_tensor("qk_parts", (2, P, 6, T), BF16, kind="Internal").ap()
        nm_d = nc.dram_tensor("minus_maxima", (NPART * H, T), BF16, kind="Internal").ap()

        def at(tensor, b):
            return tensor[b] if isinstance(b, int) else tensor[bass.ds(b, 1)].rearrange("o p t d -> (o p) t d")

        block = ctx.enter_context(nc.Block())

        def schedule(eng, body):
            for b in range(-2, 2):
                body(b, b % 2)
            with eng.Fori(1, B // 2 - 1) as pair:
                body(2 * pair, 0)
                body(2 * pair + 1, 1)
            for b in range(B - 2, B + 1):
                body(b, b % 2)

        def has(b, lo=0):
            return not isinstance(b, int) or lo <= b < B

        def all_set(eng):
            for s, n in ((blank_set, len(BLANKS) + len(ONES)), (pool_set, 9), (weights_in, 16 * len(WEIGHTS)),
                         (pad_in, 16 * len(PADDED)), (expert_sb, 6), (consts, CONSTS)):
                eng.wait_ge(s.sem, n)

        @block.sync
        def _(sp):
            for dst, src in WEIGHTS:
                sp.dma_start(dst, src, allow_slow_non_contiguous=True).then_inc(weights_in.sem, 16)
            sp.wait_ge(blank_set.sem, len(BLANKS))
            for dst, src in PADDED:
                sp.dma_start(dst, src).then_inc(pad_in.sem, 16)
            all_set(sp)

            def body(b, q):
                if has(b + 2):
                    sp.wait_ge(*done(xn_ok, b))
                    sp.dma_start(xl[:, q], at(x_d, b + 2)).then_inc(x_in.sem, 16)
                if has(b - 1):
                    sp.wait_ge(*done(ob_ok, b - 1))
                    sp.dma_start(at(o_d, b - 1), ob[:]).then_inc(out_st.sem, 16)
                if has(b):
                    sp.dma_start(xr[:], at(x_d, b)).then_inc(xr_in.sem, 16)
                if has(b + 1):
                    sp.wait_ge(*done(nmT_ok, b + 1))
                    sp.wait_ge(*done(shift_in, b))
                    sp.dma_start(nm_d, nmT[:]).then_inc(nm_out.sem, 16)
                if has(b + 2):
                    sp.wait_ge(*done(stacks_in, b + 1))
                    for n, parts in enumerate((qp, kp)):
                        sp.wait_ge(*done(qklo_ok, b + 2, n + 1))
                        for first, count in ((0, 3), (3, 2), (5, 1)):
                            src = parts[:, 0:count] if n else \
                                parts[:, 3 - count:4 - count].to_broadcast([P, count, T])
                            sp.dma_start(qk_d[n, :, first:first + count], src).then_inc(qk_out.sem, 16)
                if has(b + 1):
                    sp.wait_ge(*done(nm_out, b + 1))
                    for par in range(2):
                        sp.dma_start(qz[1 - q][64 * par + SHIFT:64 * par + SHIFT + NPART, :, par],
                                     nm_d.rearrange("(r p two) t -> two r p t", r=NPART, two=2)[par]).then_inc(shift_in.sem, 16)
                if has(b + 2):
                    sp.wait_ge(*done(sT_ps, b))
                    sp.wait_ge(*done(qk_out, b + 2))
                    for par in range(2):
                        first = 64 * par
                        sp.dma_start(qz[q][first + SHIFT:first + SHIFT + NPART, :, par],
                                     zrow[:].unsqueeze(1).to_broadcast([NPART, NPAIR, T])).then_inc(stacks_in.sem, 16)
                        for n, dst in enumerate((qz[q][first:first + SHIFT, :, par], kd[q][first:first + SHIFT])):
                            src = qk_d[n].rearrange("(p two d) c t -> two (d c) p t", two=2, d=DH)[par]
                            sp.dma_start(dst, src).then_inc(stacks_in.sem, 16)
                if has(b + 1):
                    sp.wait_ge(*done(xn_ok, b + 1))
                    sp.wait_ge(*done(x1_ok, b))
                    sp.dma_start(xnr[:], xn[:, 1 - q]).then_inc(xn_copied.sem, 16)
                    sp.wait_ge(*done(xc_ok, b + 1))
                    sp.wait_ge(*done(z_ok, b))
                    sp.dma_start(xcr[:], xc[:, 1 - q]).then_inc(xc_copied.sem, 16)

            schedule(sp, body)
            sp.wait_ge(*done(out_st, B - 1))

        @block.tensor
        def _(pe):
            pe.wait_ge(blank_set.sem, len(BLANKS) + len(ONES))
            pe.wait_ge(pool_set.sem, 9)
            pe.wait_ge(weights_in.sem, 16 * len(WEIGHTS))
            for k in range(6):
                for c in range(4):
                    if k < 4:
                        src = m1raw[:, 2 * k + c // 2, c % 2, :]
                    else:
                        src = m2raw[:, 4 * (k - 4) + c, :]
                    mm = nc.tensor.transpose(bank_bf(k)[:, P * c:P * (c + 1)], src, identb[:])
                mm.then_inc(expert_ps.sem, 1)
            all_set(pe)

            def score_t(b, q, n):
                g, j = n // NT, n % NT
                if n == 0:
                    pe.wait_ge(*done(stacks_in, b))
                    pe.wait_ge(*done(shift_in, b))
                if n >= 2:
                    pe.wait_ge(*done(exp_ok, b, n - 1))
                else:
                    pe.wait_ge(*done(hid_ok, b - 1))
                    if isinstance(b, int) and b == 0:
                        for s in (st_ok, qkr_ok, v_ok):
                            pe.wait_ge(*done(s, b + 1))
                w_q = 2 * P if j < NT - 1 else P
                for pr in range(2):
                    p = 2 * g + pr
                    o = bank(2 * (n % 2) + pr).rearrange("p (r q) -> p r q", r=2)[:, :, 0:w_q]
                    mm = nc.tensor.matmul(o, kd[q][:, p, P * j:P * (j + 1)], qz[q][:, p, :, P * j:P * j + w_q],
                                          start=True, stop=True)
                mm.then_inc(sT_ps.sem, 1)

            def score(b, q, n, pr):
                g, i = n // NT, n % NT
                if n == 0:
                    pe.wait_ge(*done(stacks_in, b))
                    pe.wait_ge(*done(gc_ok, b - 2, E))
                    pe.wait_ge(*done(gpre_ok, b))
                else:
                    pe.wait_ge(*done(mx_ok, b, 2 * n - 1 + pr))
                lo = 0 if i else P
                o = bank(4 + pr).rearrange("p (r k) -> p r k", r=2)
                p = 2 * g + pr
                for par in range(2):
                    nc.tensor.matmul(o[:, par, lo:], qz[q][:, p, par, P * i:P * (i + 1)],
                                     kd[q][:, p, P * (i - 1) + lo:P * (i + 1)], start=par == 0, stop=False,
                                     skip_group_check=True)
                nc.tensor.matmul(o[:, :, lo:], identb[:], mask[:, :, lo:], start=False, stop=True,
                                 skip_group_check=True).then_inc(s_ps.sem, 1)

            def values(b, q, n):
                g, j = n // NT, n % NT
                pe.wait_ge(*done(pt_ok, b, n + 1))
                if n == 0:
                    pe.wait_ge(*done(v_ok, b))
                    pe.wait_ge(*done(s_ok, b - 1))
                    if isinstance(b, int) and b == 0:
                        pe.wait_ge(*done(lg_ok, b + 1))
                elif j == 0:
                    pe.wait_ge(*done(ot_ok, b, g))
                w_q = 2 * P if j < NT - 1 else P
                for c in range(HG):
                    mm = nc.tensor.matmul(ps[32 * c:32 * (c + 1), 6, P * j:P * j + w_q], va[:, q, j, HG * g + c, :],
                                          pt[:, n % NPT, c, 0:w_q], start=j == 0, stop=True,
                                          skip_group_check=True)
                mm.then_inc(pv_ps.sem, 1)

            def turn_out(b, g):
                pe.wait_ge(*done(ot_ok, b, g + 1))
                if g == 0:
                    pe.wait_ge(*done(cb_ok, b - 1))
                else:
                    pe.wait_ge(*done(ao_ok, b, g))
                for t in range(NT):
                    mm = nc.tensor.transpose(bank_t(7)[:, t], ot[:, P * t:P * (t + 1)], ident[:])
                mm.then_inc(ott_ps.sem, 1)

            def turn4(k, src):
                for t in range(NT):
                    mm = nc.tensor.transpose(k[:, P * t:P * (t + 1)], src(t), identb[:] if src(t).dtype == BF16 else ident[:])
                return mm

            def body(b, q):
                main, nxt, nx2 = has(b), has(b + 1), has(b + 2)
                for n in range(NCH + 4):
                    if nxt and n < NCH:
                        score(b + 1, 1 - q, n, 0)
                    if main and n < NCH:
                        score_t(b, q, n)
                    if nxt and n < NCH:
                        score(b + 1, 1 - q, n, 1)
                    if main and 3 <= n < NCH + 3:
                        values(b, q, n - 3)
                    if main and n >= 7 and (n - 7) % NT == 0 and n < NCH + 3:
                        turn_out(b, (n - 7) // NT)
                    if nx2 and n == NCH:
                        pe.wait_ge(*done(h0_ok, b + 2))
                        if main:
                            pe.wait_ge(*done(exp_ok, b, NCH))
                        else:
                            for s in (st_ok, qkr_ok, v_ok):
                                pe.wait_ge(*done(s, b + 1))
                        turn4(bank(0), lambda t: h0[:, t]).then_inc(hT_ps.sem, 1)
                    if nx2 and n == NCH + 2:
                        pe.wait_ge(*done(hT_ok, b + 2))
                        nc.tensor.matmul(bank(1), wq[:], hT[:], start=True, stop=True).then_inc(q_ps.sem, 1)
                        nc.tensor.matmul(bank(2), wk[:], hT[:], start=True, stop=True).then_inc(k_ps.sem, 1)
                if main:
                    turn_out(b, NG - 1)
                if nx2:
                    nc.tensor.matmul(bank(0), bw[:], hT[:], start=True, stop=True).then_inc(u_ps.sem, 1)
                    for t in range(NT):
                        mm = nc.tensor.matmul(bank_t(3)[:, t], hT[:, P * t:P * (t + 1)], wv[:], start=True, stop=True)
                    mm.then_inc(v_ps.sem, 1)
                if nxt:
                    pe.wait_ge(*done(nm_step, b + 1))
                    apart(pe, b)
                    for t in range(NT):
                        mm = nc.tensor.transpose(bank_bf(5)[0:NPART * H, P * t:P * (t + 1)], nm[:, t].rearrange("p r h -> p (r h)"), identb[:])
                    mm.then_inc(nm_ps.sem, 1)
                    pe.wait_ge(*done(route, b + 1))
                    turn4(bank_bf2(5), lambda t: cp[:, t]).then_inc(cT_ps.sem, 1)
                if nx2:
                    if not main:
                        pe.wait_ge(*done(gpre_ok, b + 1))
                    for t in range(NT):
                        mm = nc.tensor.matmul(bank_t(4)[:, t], hT[:, P * t:P * (t + 1)], wg[:], start=True, stop=True)
                    mm.then_inc(g_ps.sem, 1)
                if main:
                    pe.wait_ge(*done(st_ok, b))
                    if nxt:
                        for s in (nmT_ok, cT_ok):
                            pe.wait_ge(*done(s, b + 1))
                    for t in range(NT):
                        nc.tensor.matmul(bank_t(5)[:, t], st[:, q, P * t:P * (t + 1)], cw[:], start=True, stop=True)
                    for t in range(NT):
                        mm = nc.tensor.matmul(bank_t(6)[:, t], st[:, q, P * t:P * (t + 1)], ncw[:], start=t == 0, stop=False,
                                              skip_group_check=True)
                    mm.then_inc(cw_ps.sem, 1)
                    pe.wait_ge(*done(ao_ok, b, NG))
                    turn4(bank(7), lambda t: ao[:, t]).then_inc(aoT_ps.sem, 1)

                def up(e):
                    k = 3 * (e % 2)
                    if e < 2 and nx2:
                        for s in ((st_ok, qkr_ok), (v_ok, gpre_ok))[e]:
                            pe.wait_ge(*done(s, b + 2))
                    if e == 1:
                        pe.wait_ge(*done(s1_ok, b))
                    elif e >= 2:
                        pe.wait_ge(*done(ga_ok, b, e - 1))
                        pe.wait_ge(*done(gc_ok, b, e - 1))
                    for s in range(2):
                        nc.tensor.matmul(bank(k + s), m1[:, e, s], nfT[:, q], start=True, stop=True)
                    nc.tensor.matmul(bank(k + 2), sel[:, e], cT[:, q], start=True, stop=True).then_inc(up_ps.sem, 1)

                def down(e):
                    pe.wait_ge(*done(act_ok, b, e + 1))
                    for t in range(NT):
                        mm = nc.tensor.matmul(bank_t(7)[:, t], act_t[:, e % 3, P * t:P * (t + 1)], m2[:, e], start=False,
                                              stop=e == E - 1, skip_group_check=True)
                    mm.then_inc(down_ps.sem, 1)

                def router():
                    turn4(bank_bf(6), lambda t: nf[:, t]).then_inc(nfT_ps.sem, 1)

                def logits():
                    pe.wait_ge(*done(nfn_ok, b + 2))
                    for t in range(NT):
                        mm = nc.tensor.matmul(bank(6)[:, T // 2 + E * t:T // 2 + E * (t + 1)], nfn[:, P * t:P * (t + 1)], gw[:], start=True, stop=True)
                    mm.then_inc(lg_ps.sem, 1)

                def mlp_up(j):
                    if j == 0:
                        pe.wait_ge(*done(h2T_ok, b))
                    elif j == 1:
                        pe.wait_ge(*done(ga_ok, b, E - 1))
                    elif j == 3:
                        pe.wait_ge(*done(gc_ok, b, E - 1))
                    nc.tensor.matmul(bank((6, 0, 1, 2)[j]), w1[:, P * j:P * (j + 1)], h2T[:], start=True, stop=True).then_inc(w1_ps.sem, 1)

                if main:
                    pe.wait_ge(*done(nfT_ok, b))
                    up(0)
                    pe.wait_ge(*done(aoT_ok, b))
                    for t in range(NT):
                        mm = nc.tensor.matmul(bank_t(6)[:, t], aoT[:, P * t:P * (t + 1)], wo[:], start=False, stop=True,
                                              skip_group_check=True)
                    mm.then_inc(wo_ps.sem, 1)
                    up(1)
                    for t in range(NT):
                        nc.tensor.matmul(bank_t(7)[:, t], cT[:, q, P * t:P * (t + 1)], b2st[:], start=t == 0,
                                         stop=False, skip_group_check=True)
                    for e in range(2, E):
                        if e == 6:
                            pe.wait_ge(*done(h2_ok, b))
                            if nx2:
                                pe.wait_ge(*done(lg_ok, b + 2))
                            turn4(bank(6), lambda t: h2[:, t]).then_inc(h2T_ps.sem, 1)
                        up(e)
                        if nx2 and e == 3:
                            pe.wait_ge(*done(nf_ok, b + 2))
                            pe.wait_ge(*done(t1_ok, b))
                            router()
                        if nx2 and e == 4:
                            logits()
                        down(e - 2)
                    mlp_up(0)
                    mlp_up(1)
                    down(E - 2)
                    mlp_up(2)
                    mlp_up(3)
                    down(E - 1)
                    for t in range(NT):
                        for j in range(NJ):
                            if t == 0:
                                pe.wait_ge(*done(hid_ok, b, j + 1))
                            mm = nc.tensor.matmul(bank_t(6)[:, t], hid[:, j, P * t:P * (t + 1)], w2[:, j], start=j == 0, stop=j == NJ - 1)
                    mm.then_inc(w2_ps.sem, 1)
                elif nx2:
                    pe.wait_ge(*done(nf_ok, b + 2))
                    pe.wait_ge(*done(lg_ok, b + 1))
                    router()
                    logits()

            set_spare(pe, "pe_waited")
            schedule(pe, body)

        @block.scalar
        def _(act):
            for k in range(6):
                act.wait_ge(expert_ps.sem, k + 1)
                dst = m1[:, 2 * k:2 * k + 2].rearrange("p e s i -> p (e s i)") if k < 4 else \
                    m2[:, 4 * (k - 4):4 * (k - 3)].rearrange("p e d -> p (e d)")
                nc.scalar.activation(dst, bank_bf(k), ACT.Copy).then_inc(expert_sb.sem, 1)
            all_set(act)

            def body(b, q):
                main, nxt, nx2 = has(b), has(b + 1), has(b + 2)
                if has(b - 1):
                    act.wait_ge(*done(z_ok, b - 1))
                    act.wait_ge(*done(w_ok, b - 2))
                    nc.scalar.activation(zth[:], z[:], ACT.Tanh, scale=0.5).then_inc(zth_ok.sem, 1)
                if nxt:
                    act.wait_ge(*done(gpre_ok, b + 1))
                    act.wait_ge(*done(x1_ok, b - 1))
                    nc.scalar.activation(gth[:, 1 - q], gpre[:], ACT.Tanh, scale=0.5).then_inc(gth_ok.sem, 1)
                for n in range(NCH + 4):
                    if main and n < NCH:
                        act.wait_ge(*done(sT_ps, b, n + 1))
                        if n >= NPT:
                            act.wait_ge(*done(pv_ps, b, n - NPT + 1))
                        else:
                            act.wait_ge(*done(pv_ps, b - 1, NCH - NPT + n + 1))
                        w_q = 2 * P if n % NT < NT - 1 else P
                        src = ps[:, 2 * (n % 2):2 * (n % 2) + 2, :].rearrange("p c (r q) -> p (c r) q", r=2)[:, :, 0:w_q]
                        nc.scalar.activation(pt[:, n % NPT, :, 0:w_q], src, ACT.Exp, scale=SCALE).then_inc(exp_ok.sem, 1)
                    if main and n >= 6 and (n - 6) % NT == 0:
                        g = (n - 6) // NT
                        act.wait_ge(*done(pv_ps, b, NT * (g + 1)))
                        act.wait_ge(*done(ott_ps, b, g))
                        nc.scalar.activation(ot[:], bank(6), ACT.Copy).then_inc(ot_ok.sem, 1)
                    if nx2 and n == 7:
                        act.wait_ge(*done(xn_ok, b + 2))
                        act.wait_ge(*done(xc_copied, b))
                        nc.scalar.activation(xc[:, q], xn[:, q], ACT.Copy).then_inc(xc_ok.sem, 1)
                    if nx2 and 10 <= n < 10 + NT:
                        t = n - 10
                        act.wait_ge(*done(r2_step, b + 2))
                        act.wait_ge(*done(hT_ps, b + 1))
                        nc.scalar.activation(h0[:, t], xn[:, q, t], ACT.Copy, scale=r2[:, t:t + 1]).then_inc(h0_ok.sem, 1)
                    if nxt and n == 1:
                        act.wait_ge(*done(route, b + 1, 4))
                        nc.scalar.activation(ex[:], ld[:], ACT.Exp).then_inc(ex_ok.sem, 1)
                    if nx2 and n == NCH:
                        act.wait_ge(*done(hT_ps, b + 2))
                        act.wait_ge(*done(g_ps, b + 1))
                        nc.scalar.activation(hT[:], bank(0), ACT.Identity, bias=cols["ln1_b"][:], scale=cols["ln1_g"][:]).then_inc(hT_ok.sem, 1)
                if nx2:
                    act.wait_ge(*done(stacks_in, b + 1))
                    for n, (signal_ps, dst, bias) in enumerate(((q_ps, qp, "bQ"), (k_ps, kp, "bK"))):
                        act.wait_ge(*done(signal_ps, b + 2))
                        nc.scalar.activation(dst[:, 0], bank(1 + n), ACT.Identity, bias=cols[bias][:]).then_inc(qkhi_ok.sem, 1)
                if nxt:
                    act.wait_ge(*done(nm_ps, b + 1))
                    act.wait_ge(*done(cT_ps, b + 1))
                    act.wait_ge(*done(shift_in, b))
                    nc.scalar.activation(nmT[:], bank_bf(5)[0:NPART * H, :], ACT.Copy).then_inc(nmT_ok.sem, 1)
                    act.wait_ge(*done(down_ps, b - 1))
                    nc.scalar.activation(cT[:, 1 - q], bank_bf2(5), ACT.Copy).then_inc(cT_ok.sem, 1)
                def router_in():
                    act.wait_ge(*done(nfT_ps, b + 2))
                    act.wait_ge(*done(nfT_ok, b + 1))
                    act.wait_ge(*done(lg_ps, b + 1))
                    nc.scalar.activation(nfn[:], bank_bf(6), ACT.Copy).then_inc(nfn_ok.sem, 1)

                if main:
                    act.wait_ge(*done(aoT_ps, b))
                    act.wait_ge(*done(wo_ps, b - 1))
                    nc.scalar.activation(aoT[:], bank(7), ACT.Copy).then_inc(aoT_ok.sem, 1)
                    for e in range(E):
                        act.wait_ge(*done(up_ps, b, e + 1))
                        if e >= 2:
                            act.wait_ge(*done(gc_ok, b, e - 1))
                        else:
                            act.wait_ge(*done(gc_ok, b - 1))
                        if e >= 2:
                            act.wait_ge(*done(act_ok, b, e - 1))
                        else:
                            act.wait_ge(*done(act_ok, b - 1))
                        nc.scalar.activation(lin[:, e % 2], bank(3 * (e % 2) + 1), ACT.Identity, bias=mbias[:, e, 1:2]).then_inc(lin_ok.sem, 1)
                        nc.scalar.activation(ga[:, e % 2], bank(3 * (e % 2)), ACT.Gelu_apprx_sigmoid, bias=mbias[:, e, 0:1]).then_inc(ga_ok.sem, 1)
                        if nx2 and e == 3:
                            router_in()
                        if e == 6:
                            act.wait_ge(*done(h2T_ps, b))
                            act.wait_ge(*done(w1_ps, b - 1))
                            nc.scalar.activation(h2T[:], bank(6), ACT.Identity, bias=cols["ln2_b"][:], scale=cols["ln2_g"][:]).then_inc(h2T_ok.sem, 1)
                    for j, k in enumerate((6, 0, 1, 2)):
                        act.wait_ge(*done(w1_ps, b, j + 1))
                        if j == 0:
                            act.wait_ge(*done(w2_ps, b - 1))
                        nc.scalar.activation(hid[:, j], bank(k), ACT.Gelu, bias=b1c[:, j:j + 1]).then_inc(hid_ok.sem, 1)
                    act.wait_ge(*done(down_ps, b))
                    act.wait_ge(*done(z_ok, b - 1))
                    nc.scalar.activation(cb[:], bank_t(7), ACT.Copy).then_inc(cb_ok.sem, 1)
                elif nx2:
                    router_in()

            schedule(act, body)

        @block.vector
        def _(dve):
            for dst, value in BLANKS:
                nc.vector.memset(dst, value).then_inc(blank_set.sem, 1)
            dve.wait_ge(blank_set.sem, len(BLANKS))
            for dst, value in ONES:
                nc.vector.memset(dst, value).then_inc(blank_set.sem, 1)
            dve.wait_ge(weights_in.sem, 16 * len(WEIGHTS))
            dve.wait_ge(pad_in.sem, 16 * len(PADDED))
            nc.vector.tensor_scalar(ncw[0:N, :], cw[0:N, :], -1.0, None, ALU.mult).then_inc(consts.sem, 1)
            nc.vector.tensor_copy(mbias[:, :, 0:1], mb_b[:, :, 0:1]).then_inc(consts.sem, 1)
            nc.vector.tensor_scalar(mbias[:, :, 1:2], mb_b[:, :, 1:2], 1.0, None, ALU.add).then_inc(consts.sem, 1)
            nc.vector.tensor_copy(gbias[:], gbias_b[:]).then_inc(consts.sem, 1)
            all_set(dve)

            def finish(b, part):
                if part == 0:
                    dve.wait_ge(*done(zth_ok, b))
                    nc.vector.scalar_tensor_tensor(out=zth[:], in0=zth[:], scalar=1.0, in1=z[:], op0=ALU.add, op1=ALU.mult).then_inc(y_ok.sem, 1)
                else:
                    dve.wait_ge(*done(y_ok, b))
                    dve.wait_ge(*done(s_ok, b))
                    nc.vector.scalar_tensor_tensor(out=sres[:], in0=zth[:], scalar=0.5, in1=sres[:], op0=ALU.mult, op1=ALU.mult).then_inc(w_ok.sem, 1)

            def norm_stats(b, q, tiles):
                if tiles[0] == 0:
                    dve.wait_ge(*done(x_in, b))
                    dve.wait_ge(*done(mv_ok, b - 1))
                for t in tiles:
                    bn = nc.vector.bn_stats(stats[:, t], xl[:, q, t])
                bn.then_inc(stats_ok.sem, 1)

            def norm_moments(b):
                dve.wait_ge(*done(stats_ok, b))
                dve.wait_ge(*done(xn_ok, b - 1))
                apart(dve, b)
                for t in range(NT):
                    bn = nc.vector.bn_aggr(mv[:, t], stats[:, t])
                bn.then_inc(mv_ok.sem, 1)

            def norm_x(b, q, tiles):
                if tiles[0] == 0:
                    dve.wait_ge(*done(r1_step, b))
                    dve.wait_ge(*done(xn_copied, b - 2))
                for t in tiles:
                    ts = nc.vector.tensor_scalar(xn[:, q, t], xl[:, q, t], mv[:, t, 0:1], r1[:, t:t + 1], ALU.subtract, ALU.mult)
                ts.then_inc(xn_ok.sem, 1)

            def squares(b, q, tiles):
                if tiles[0] == 0:
                    dve.wait_ge(*done(xc_ok, b))
                    dve.wait_ge(*done(rs_step, b - 1))
                for t in tiles:
                    tr = nc.vector.tensor_tensor_reduce(junk[:, t], xc[:, q, t], xc[:, q, t], 1.0, 0.0, ALU.mult, ALU.add, sq[:, t:t + 1])
                tr.then_inc(sq_ok.sem, 1)

            def norm_f(b, q, tiles):
                if tiles[0] == 0:
                    dve.wait_ge(*done(rs_step, b))
                    dve.wait_ge(*done(nfT_ps, b - 1))
                for t in tiles:
                    ts = nc.vector.scalar_tensor_tensor(out=nf[:, t], in0=xc[:, q, t], scalar=rs[:, t:t + 1], in1=rows["nw"][:],
                                                        op0=ALU.mult, op1=ALU.mult)
                ts.then_inc(nf_ok.sem, 1)

            def route_rank(b):
                dve.wait_ge(*done(lg_ok, b))
                shape = [P, NT, E, E]
                nc.vector.tensor_tensor(dl[:], lg[:].unsqueeze(2).to_broadcast(shape), lg[:].unsqueeze(3).to_broadcast(shape),
                                        ALU.subtract).then_inc(route.sem, 1)
                nc.vector.tensor_reduce(lmax[:], lg[:], AX.X, ALU.max).then_inc(route.sem, 1)
                dve.wait_ge(*done(route, b, 2))
                nc.vector.tensor_tensor(bt[:], dl[:], tie[:].unsqueeze(1).to_broadcast(shape), ALU.is_gt).then_inc(route.sem, 1)
                nc.vector.tensor_tensor(ld[:], lg[:], lmax[:].unsqueeze(2).to_broadcast([P, NT, E]), ALU.subtract).then_inc(route.sem, 1)
                dve.wait_ge(*done(route, b, 4))
                nc.vector.tensor_reduce(rank[:], bt[:], AX.X, ALU.add).then_inc(route.sem, 1)

            def route_mix(b, part):
                if part == 0:
                    dve.wait_ge(*done(route, b, 5))
                    dve.wait_ge(*done(ex_ok, b))
                    nc.vector.scalar_tensor_tensor(out=exs[:], in0=rank[:], scalar=2.0, in1=ex[:], op0=ALU.is_lt, op1=ALU.mult).then_inc(route.sem, 1)
                    dve.wait_ge(*done(route, b, 6))
                    nc.vector.tensor_reduce(zs[:], exs[:], AX.X, ALU.add).then_inc(route.sem, 1)
                elif part == 1:
                    dve.wait_ge(*done(route, b, 7))
                    nc.vector.reciprocal(zr[:], zs[:]).then_inc(route.sem, 1)
                    dve.wait_ge(*done(route, b, 8))
                    nc.vector.tensor_tensor(cmb[:], exs[:], zr[:].unsqueeze(2).to_broadcast([P, NT, E]), ALU.mult).then_inc(route.sem, 1)
                elif part == 2:
                    dve.wait_ge(*done(route, b, 9))
                    dve.wait_ge(*done(cT_ps, b - 1))
                    nc.vector.tensor_copy(cp[:, :, 0:E], cmb[:]).then_inc(route.sem, 1)
                    dve.wait_ge(*done(route, b, 10))
                    nc.vector.tensor_tensor(cr[:], cmb[:], cp[:, :, 0:E], ALU.subtract).then_inc(route.sem, 1)
                else:
                    dve.wait_ge(*done(route, b, 11))
                    nc.vector.tensor_copy(cp[:, :, E:2 * E], cr[:]).then_inc(route.sem, 1)
                    dve.wait_ge(*done(route, b, 12))
                    nc.vector.tensor_tensor(cp[:, :, 2 * E:3 * E], cr[:], cp[:, :, E:2 * E], ALU.subtract).then_inc(route.sem, 1)

            def body(b, q):
                main, nxt, nx2 = has(b), has(b + 1), has(b + 2)

                def logits_in():
                    dve.wait_ge(*done(lg_ps, b + 2))
                    dve.wait_ge(*done(route, b + 1))
                    nc.vector.tensor_tensor(lg[:], bank(6)[:, T // 2:T // 2 + NT * E].rearrange("p (t e) -> p t e", e=E),
                                            gbias[:].unsqueeze(1).to_broadcast([P, NT, E]), ALU.add).then_inc(lg_ok.sem, 1)

                for n in range(NCH + 5):
                    g, i = n // NT, n % NT
                    for pr in range(2):
                        step = 2 * n + pr
                        if nxt and n < NCH:
                            lo = 0 if i else P
                            dve.wait_ge(*done(s_ps, b + 1, step + 1))
                            if n == 0:
                                dve.wait_ge(*done(nm_step, b))
                            src = bank(4 + pr).rearrange("p (r k) -> p r k", r=2)[:, :, lo:]
                            h = HG * g + 2 * pr
                            nc.vector.tensor_reduce(mx[:, i, h:h + 2], src, AX.X, ALU.max).then_inc(mx_ok.sem, 1)
                        if has(b - 1) and step in (1, 3):
                            finish(b - 1, step // 2)
                        if nx2:
                            if step in (5, 6):
                                norm_stats(b + 2, q, (0, 1) if step == 5 else (2, 3))
                            if step == 7:
                                norm_moments(b + 2)
                            if step in (12, 13):
                                norm_x(b + 2, q, (0, 1) if step == 12 else (2, 3))
                            if step in (18, 19):
                                squares(b + 2, q, (0, 1) if step == 18 else (2, 3))
                            if step in (26, 28):
                                norm_f(b + 2, q, (0, 1) if step == 26 else (2, 3))
                        if nxt and 8 <= step < 12:
                            route_mix(b + 1, step - 8)
                    if nxt and n == NCH:
                        dve.wait_ge(*done(mx_ok, b + 1))
                        dve.wait_ge(*done(nm_ps, b))
                        nc.vector.tensor_scalar(nm[:, :, 0], mx[:], -1.0, None, ALU.mult).then_inc(nm_step.sem, 1)
                        dve.wait_ge(*done(nm_step, b + 1, 1))
                        nc.vector.scalar_tensor_tensor(out=mr[:], in0=mx[:], scalar=-1.0, in1=nm[:, :, 0], op0=ALU.mult, op1=ALU.subtract).then_inc(nm_step.sem, 1)
                        dve.wait_ge(*done(nm_step, b + 1, 2))
                        nc.vector.tensor_copy(nm[:, :, 1], mr[:]).then_inc(nm_step.sem, 1)
                        dve.wait_ge(*done(nm_step, b + 1, 3))
                        nc.vector.tensor_tensor(nm[:, :, 2], mr[:], nm[:, :, 1], ALU.subtract).then_inc(nm_step.sem, 1)
                    if main and n >= 8 and (n - 8) % NT == 0:
                        g = (n - 8) // NT
                        dve.wait_ge(*done(ott_ps, b, g + 1))
                        if g == 0:
                            dve.wait_ge(*done(aoT_ps, b - 1))
                        o = bank_t(7).rearrange("p t (h v) -> p t h v", v=VW)
                        dve.wait_ge(*done(ao_ok, b, g))
                        nc.vector.reciprocal(rz[:], o[:, :, :, DH]).then_inc(rz_ok.sem, 1)
                        dve.wait_ge(*done(rz_ok, b, g + 1))
                        nc.vector.tensor_tensor(ao[:, :, HG * DH * g:HG * DH * (g + 1)].rearrange("p t (h v) -> p t h v", v=DH),
                                                o[:, :, :, 0:DH], rz[:].unsqueeze(3).to_broadcast([P, NT, HG, DH]), ALU.mult).then_inc(ao_ok.sem, 1)
                if nx2:
                    for n, (hi, rest, bias) in enumerate(((qp, qr, "bQ"), (kp, kr, "bK"))):
                        dve.wait_ge(*done(qkhi_ok, b + 2, n + 1))
                        dve.wait_ge(*done(qklo_ok, b + 1, n + 1))
                        nc.vector.scalar_tensor_tensor(out=rest[:], in0=bank(1 + n), scalar=cols[bias][:], in1=hi[:, 0],
                                                       op0=ALU.add, op1=ALU.subtract).then_inc(qkr_ok.sem, 1)
                    dve.wait_ge(*done(v_ps, b + 2))
                    dve.wait_ge(*done(pv_ps, b))
                    shape = [P, NT, H, DH]
                    nc.vector.tensor_tensor(va[:, q, :, :, 0:DH], bank_t(3).rearrange("p t (h v) -> p t h v", v=DH),
                                            rows["bV"][:].rearrange("p (h v) -> p h v", v=DH).unsqueeze(1).to_broadcast(shape), ALU.add).then_inc(v_ok.sem, 1)
                    dve.wait_ge(*done(g_ps, b + 2))
                    dve.wait_ge(*done(gth_ok, b + 1))
                    nc.vector.tensor_tensor(gpre[:], bank_t(4), rows["bg"][:].unsqueeze(1).to_broadcast([P, NT, D]), ALU.add).then_inc(gpre_ok.sem, 1)
                if nx2:
                    dve.wait_ge(*done(u_ps, b + 2))
                    dve.wait_ge(*done(cw_ps, b))
                    nc.vector.tensor_tensor_scan(st[0:N, q], acol[0:N, :].to_broadcast([N, T]), bank(0)[0:N], 0.0, ALU.mult, ALU.add).then_inc(st_ok.sem, 1)
                if main:
                    dve.wait_ge(*done(cw_ps, b))
                    dve.wait_ge(*done(xn_copied, b))
                    nc.vector.tensor_tensor(s1[:], bank_t(5), xnr[:], ALU.add).then_inc(s1_ok.sem, 1)
                    for e in range(E):
                        k = 3 * (e % 2)
                        dve.wait_ge(*done(up_ps, b, e + 1))
                        dve.wait_ge(*done(lin_ok, b, e + 1))
                        nc.vector.tensor_scalar(lin[:, e % 2], lin[:, e % 2], 1.0 - LIMIT, 1.0 + LIMIT, ALU.max, ALU.min).then_inc(clip_ok.sem, 1)
                        dve.wait_ge(*done(ga_ok, b, e + 1))
                        if e >= 2:
                            dve.wait_ge(*done(act_ok, b, e - 1))
                        nc.vector.scalar_tensor_tensor(out=gc[:, e % 2], in0=ga[:, e % 2], scalar=G_LIMIT, in1=bank(k + 2),
                                                       op0=ALU.min, op1=ALU.mult).then_inc(gc_ok.sem, 1)
                        dve.wait_ge(*done(gc_ok, b, e + 1))
                        if e >= 3:
                            dve.wait_ge(*done(down_ps, b, e - 2))
                        else:
                            dve.wait_ge(*done(down_ps, b - 1))
                        dve.wait_ge(*done(clip_ok, b, e + 1))
                        nc.vector.tensor_tensor(act_t[:, e % 3], lin[:, e % 2], gc[:, e % 2], ALU.mult).then_inc(act_ok.sem, 1)
                        if e == 0:
                            dve.wait_ge(*done(wo_ps, b))
                            dve.wait_ge(*done(gth_ok, b))
                            dve.wait_ge(*done(x1b_ok, b - 1))
                            dve.wait_ge(*done(h2_ok, b - 1))
                            nc.vector.scalar_tensor_tensor(out=x1[:], in0=gth[:, q], scalar=1.0, in1=bank_t(6), op0=ALU.add, op1=ALU.mult).then_inc(t1_ok.sem, 1)
                            dve.wait_ge(*done(t1_ok, b))
                            dve.wait_ge(*done(s1_ok, b))
                            nc.vector.scalar_tensor_tensor(out=x1[:], in0=x1[:], scalar=0.5, in1=s1[:], op0=ALU.mult, op1=ALU.add).then_inc(x1_ok.sem, 1)
                        if e == 1:
                            dve.wait_ge(*done(x1_ok, b))
                            for t in range(NT):
                                bn = nc.vector.bn_stats(st2[:, t], x1[:, t])
                            bn.then_inc(st2_ok.sem, 1)
                            dve.wait_ge(*done(st2_ok, b))
                            apart(dve, b)
                            for t in range(NT):
                                bn = nc.vector.bn_aggr(mv2[:, t], st2[:, t])
                            bn.then_inc(mv2_ok.sem, 1)
                        if e == 4:
                            dve.wait_ge(*done(r3_step, b))
                            dve.wait_ge(*done(h2T_ps, b - 1))
                            for t in range(NT):
                                ts = nc.vector.tensor_scalar(h2[:, t], x1[:, t], mv2[:, t, 0:1], r3[:, t:t + 1], ALU.subtract, ALU.mult)
                            ts.then_inc(h2_ok.sem, 1)
                        if nx2 and e == 5:
                            logits_in()
                elif nx2:
                    logits_in()
                if nx2:
                    dve.wait_ge(*done(nfn_ok, b + 2))
                    nc.vector.tensor_copy(nfT[:, q], nfn[:]).then_inc(nfT_ok.sem, 1)
                    route_rank(b + 2)
                if main:
                    dve.wait_ge(*done(cb_ok, b))
                    dve.wait_ge(*done(xc_copied, b))
                    nc.vector.tensor_tensor(z[:], xcr[:], cb[:], ALU.add).then_inc(z_ok.sem, 1)
                if main:
                    dve.wait_ge(*done(w2_ps, b))
                    dve.wait_ge(*done(x1b_ok, b))
                    dve.wait_ge(*done(ob_ok, b - 1))
                    nc.vector.tensor_tensor(sres[:], bank_t(6), x1b[:], ALU.add).then_inc(s_ok.sem, 1)

            set_spare(dve, "dve_waited")
            schedule(dve, body)

        @block.gpsimd
        def _(pool):
            pool.wait_ge(blank_set.sem, len(BLANKS))
            sg = lambda i: i.then_inc(pool_set.sem, 1)
            for m in (ident, identb):
                sg(nc.gpsimd.affine_select(out=m[:], in_=m[:], compare_op=ALU.not_equal, fill=1.0, base=0, pattern=[[-1, P]], channel_multiplier=1))
            sg(nc.gpsimd.affine_select(out=mask[:, :, 0:P], in_=mask[:, :, 0:P], compare_op=ALU.is_ge, fill=NEG, base=-1, pattern=[[0, 2], [1, P]], channel_multiplier=-1))
            sg(nc.gpsimd.affine_select(out=mask[:, :, P:], in_=mask[:, :, P:], compare_op=ALU.is_ge, fill=NEG, base=0, pattern=[[0, 2], [-1, P]], channel_multiplier=1))
            sg(nc.gpsimd.affine_select(out=tie[:], in_=tie[:], compare_op=ALU.is_ge, fill=TIE, base=0, pattern=[[-1, E], [1, E]], channel_multiplier=0))
            for c in range(NPART):
                if c:
                    pool.wait_ge(pool_set.sem, 5 + c)
                sg(nc.gpsimd.affine_select(out=sel[:], in_=sel[:], compare_op=ALU.not_equal, fill=1.0, base=-E * c, pattern=[[-1, E], [0, P]], channel_multiplier=1))
            sg(nc.gpsimd.tensor_copy(vt[:], half[:]))
            all_set(pool)

            def inv_root(dst, tmp, src, scale, step, b, first, free):
                for s, sb_, c in free:
                    pool.wait_ge(*done(s, sb_, c))
                apart(pool, b)
                nc.gpsimd.tensor_scalar(tmp, src, scale, EPS, ALU.mult, ALU.add).then_inc(step.sem, 1)
                pool.wait_ge(*done(step, b, first + 1))
                nc.gpsimd.tensor_tensor(dst, tmp, half[:], ALU.pow).then_inc(step.sem, 1)

            def body(b, q):
                main, nxt, nx2 = has(b), has(b + 1), has(b + 2)
                for n in range(NCH + 1):
                    if main and n < NCH:
                        s = n % NPT
                        pool.wait_ge(*done(exp_ok, b, n + 1))
                        apart(pool, b)
                        sel1 = nc.gpsimd.affine_select(out=pt[:, s, :, 0:P], in_=pt[:, s, :, 0:P], compare_op=ALU.is_ge, fill=0.0, base=0,
                                                       pattern=[[0, HG], [1, P]], channel_multiplier=-1)
                        if n % NT < NT - 1:
                            sel1 = nc.gpsimd.affine_select(out=pt[:, s, :, P:], in_=pt[:, s, :, P:], compare_op=ALU.is_ge, fill=0.0, base=-1,
                                                           pattern=[[0, HG], [-1, P]], channel_multiplier=1)
                        sel1.then_inc(pt_ok.sem, 1)
                    if n == 1 and has(b - 1):
                        pool.wait_ge(*done(w_ok, b - 1))
                        pool.wait_ge(*done(xr_in, b - 1))
                        pool.wait_ge(*done(out_st, b - 2))
                        nc.gpsimd.tensor_tensor(ob[:], sres[:], xr[:], ALU.add).then_inc(ob_ok.sem, 1)
                    if nx2 and n == 4:
                        pool.wait_ge(*done(mv_ok, b + 2))
                        inv_root(r1[:], r1t[:], mv[:, :, 1], 1.0, r1_step, b + 2, 0, ((xn_ok, b + 1, None),))
                    if nx2 and n == 6:
                        pool.wait_ge(*done(r1_step, b + 2))
                        nc.gpsimd.tensor_tensor(vv[:], mv[:, :, 1], r1[:], ALU.mult).then_inc(r2_step.sem, 1)
                        pool.wait_ge(*done(r2_step, b + 2, 1))
                        nc.gpsimd.tensor_tensor(vt[:], vv[:], r1[:], ALU.mult).then_inc(r2_step.sem, 1)
                        pool.wait_ge(*done(r2_step, b + 2, 2))
                        inv_root(r2[:], v2t[:], vt[:], 1.0, r2_step, b + 2, 2, ((h0_ok, b + 1, None),))
                    if nx2 and n == 10:
                        pool.wait_ge(*done(sq_ok, b + 2))
                        inv_root(rs[:], sqm[:], sq[:], 1.0 / D, rs_step, b + 2, 0, ((nf_ok, b + 1, None),))
                if nx2:
                    for n, (parts, rest) in enumerate(((qp, qr), (kp, kr))):
                        pool.wait_ge(*done(qkr_ok, b + 2, n + 1))
                        apart(pool, b)
                        nc.gpsimd.tensor_scalar(parts[:, 1], rest[:], 1.0, 0.0, ALU.mult, ALU.add).then_inc(qkmid_ok.sem, 1)
                        pool.wait_ge(*done(qkmid_ok, b + 2, n + 1))
                        nc.gpsimd.tensor_tensor(parts[:, 2], rest[:], parts[:, 1], ALU.subtract).then_inc(qklo_ok.sem, 1)
                if main:
                    pool.wait_ge(*done(mv2_ok, b))
                    inv_root(r3[:], r3t[:], mv2[:, :, 1], 1.0, r3_step, b, 0, ((h2_ok, b - 1, None),))
                    pool.wait_ge(*done(s_ok, b - 1))
                    nc.gpsimd.tensor_tensor(x1b[:], x1[:], rows["b2"][:].unsqueeze(1).to_broadcast([P, NT, D]), ALU.add).then_inc(x1b_ok.sem, 1)

            r3t = sb("r3t", [P, NT])
            set_spare(pool, "pool_waited")
            schedule(pool, body)


_NAMES = {
    "x": "L0_attn_x", "ln1_g": "L0_attn_ln1_g", "ln1_b": "L0_attn_ln1_b", "WQ": "L0_attn_WQ", "bQ": "L0_attn_bQ",
    "WK": "L0_attn_WK", "bK": "L0_attn_bK", "WV": "L0_attn_WV", "bV": "L0_attn_bV", "WO": "L0_attn_WO",
    "bO": "L0_attn_bO", "Wg": "L0_attn_Wg", "bg": "L0_attn_bg", "A": "L0_attn_A", "Bw": "L0_attn_Bw",
    "Cw": "L0_attn_Cw", "ln2_g": "L0_attn_ln2_g", "ln2_b": "L0_attn_ln2_b", "W1": "L0_attn_W1", "b1": "L0_attn_b1",
    "W2": "L0_attn_W2", "b2": "L0_attn_b2", "norm_weight": "L0_ffn_norm_weight", "gate_weight": "L0_ffn_gate_weight",
    "gate_bias": "L0_ffn_gate_bias", "mlp1_weight": "L0_ffn_mlp1_weight", "mlp1_bias": "L0_ffn_mlp1_bias",
    "mlp2_weight": "L0_ffn_mlp2_weight", "mlp2_bias": "L0_ffn_mlp2_bias",
}


def kernel(**inputs):
    import concourse.bacc as bacc
    from concourse.bass_utils import run_bass_kernel_spmd as run

    nc = bacc.Bacc("TRN2", target_bir_lowering=False, num_devices=1)
    arrays, args = {}, {}
    for short, name in _NAMES.items():
        v = np.ascontiguousarray(inputs[name])
        arrays[name] = v
        args[short] = nc.dram_tensor(name, v.shape, mybir.dt.from_np(v.dtype), kind="ExternalInput").ap()
    out = nc.dram_tensor("out", (B, T, D), F32, kind="ExternalOutput").ap()
    build(nc, args, out)
    return run(nc, [arrays], core_ids=[0]).results[0]["out"]
```

```python
from contextlib import ExitStack

import numpy as np

import concourse.bass as bass
from concourse import mybir

ALU = mybir.AluOpType
ACT = mybir.ActivationFunctionType
AX = mybir.AxisListType
F32 = mybir.dt.float32
BF16 = mybir.dt.bfloat16

B, T, D = 16, 512, 128
P = 128
NT = T // P
H, DH = 16, 8
NPAIR = H // 2
HG = 4
NG = H // HG
NCH = NG * NT
N = 64
DFF = 512
NJ = DFF // P
E, I = 8, 128
VW = 32
NPART = 3
SHIFT = 6 * DH
EPS = 1e-5
LIMIT, ALPHA = 7.0, 1.702
G_LIMIT = float(LIMIT / (1.0 + np.exp(-ALPHA * LIMIT)))
SCALE = float(1.0 / np.sqrt(np.float32(DH)))
NEG = -1e30
TIE = -1e-37
CONSTS = 4


class Signal:

    def __init__(self, sem, per):
        self.sem, self.per = sem, per


def build(nc, a, out):
    with ExitStack() as ctx:
        def sb(name, shape, dt=F32):
            return ctx.enter_context(nc.sbuf_tensor(name, shape, dt))

        def signal(name, per):
            return Signal(ctx.enter_context(nc.semaphore(name)), per)

        ps = ctx.enter_context(nc.psum_tensor("ps", [P, 8, 512], F32))

        def bank(k):
            return ps[:, k, :]

        def bank_t(k):
            return ps[:, k, :].rearrange("p (t d) -> p t d", t=NT)

        def bank_bf(k, part=0):
            return ps[:, k, :].bitcast(BF16)[:, T * part:T * (part + 1)]

        ident = sb("ident", [P, P])
        identb = sb("identb", [P, P], BF16)
        mask = sb("mask", [P, 2, 2 * P], BF16)
        sel = sb("sel", [P, E, P], BF16)
        tie = sb("tie", [P, E, E])
        half = sb("half", [P, NT])
        zrow = sb("zrow", [NPART, T], BF16)
        wq, wk, wv, wo, wg = (sb(n, [P, P]) for n in ("wq", "wk", "wv", "wo", "wg"))
        bw = sb("bw", [P, P])
        cw = sb("cw", [P, P])
        ncw = sb("ncw", [P, P])
        w1 = sb("w1", [P, DFF])
        w2 = sb("w2", [P, NJ, P])
        cols = {n: sb(n, [P, 1]) for n in ("ln1_g", "ln1_b", "bQ", "bK", "ln2_g", "ln2_b")}
        b1c = sb("b1c", [P, NJ])
        acol = sb("acol", [P, 1])
        rows = {n: sb("row_" + n, [P, P]) for n in ("bV", "bg", "b2", "nw")}
        gbias_b = sb("gbias_b", [P, E], BF16)
        gbias = sb("gbias", [P, E])
        gw = sb("gw", [P, E], BF16)
        m1 = sb("m1", [P, E, 2, P], BF16)
        m2 = sb("m2", [P, E, P])
        mb_b = sb("mb_b", [P, E, 2], BF16)
        mbias = sb("mbias", [P, E, 2])
        b2st = sb("b2st", [P, P], BF16)

        xl = sb("xl", [P, 2, NT, D])
        stats = sb("stats", [P, NT, 6])
        mv = sb("mv", [P, NT, 2])
        r1, r1t, vv, vvt, r2, r2t, sq, sqm, rs = (
            sb(n, [P, NT]) for n in ("r1", "r1t", "vv", "vvt", "r2", "r2t", "sq", "sqm", "rs"))
        xn = sb("xn", [P, 2, NT, D])
        xc = sb("xc", [P, 2, NT, D], BF16)
        junk = sb("junk", [P, NT, D], BF16)
        h0 = sb("h0", [P, NT, D])
        nf = sb("nf", [P, NT, D], BF16)
        hT = sb("hT", [P, T])
        nfT = sb("nfT", [P, 2, T], BF16)
        nfn = sb("nfn", [P, T], BF16)
        qp = sb("qp", [P, NPART, T], BF16)
        kp = sb("kp", [P, NPART, T], BF16)
        qr = sb("qr", [P, T])
        kr = sb("kr", [P, T])
        qz = [sb(f"qz{i}", [P, NPAIR, 2, T], BF16) for i in range(2)]
        kd = [sb(f"kd{i}", [P, NPAIR, T], BF16) for i in range(2)]
        va = sb("va", [P, 2, NT, H, VW])
        st = sb("st", [P, 2, T])
        gpre = sb("gpre", [P, NT, D])
        gth = sb("gth", [P, 2, NT, D])
        mx = sb("mx", [P, NT, H])
        mr = sb("mr", [P, NT, H])
        nm = sb("nm", [P, NT, NPART, H], BF16)
        nmT = sb("nmT", [NPART * H, T], BF16)
        NPT = 4
        pt = sb("pt", [P, NPT, HG, 2 * P])
        m1raw = pt[:, 0].rearrange("p h q -> p (h q)").bitcast(BF16).rearrange("p (e s h) -> p e s h", e=E, s=2)
        m2raw = pt[:, 1].rearrange("p h q -> p (h q)").bitcast(BF16)[:, 0:E * P].rearrange("p (e i) -> p e i", e=E)
        ot = sb("ot", [P, T])
        rz = sb("rz", [P, NT, HG])
        ao = sb("ao", [P, NT, H * DH])
        aoT = sb("aoT", [P, T])
        lg = sb("lg", [P, NT, E], BF16)
        dl = sb("dl", [P, NT, E, E])
        bt = sb("bt", [P, NT, E, E])
        rank = sb("rank", [P, NT, E])
        lmax = sb("lmax", [P, NT])
        ld = sb("ld", [P, NT, E])
        ex = sb("ex", [P, NT, E])
        exs = sb("exs", [P, NT, E])
        zs = sb("zs", [P, NT])
        zr = sb("zr", [P, NT])
        cmb = sb("cmb", [P, NT, E])
        cr = sb("cr", [P, NT, E])
        cp = sb("cp", [P, NT, P], BF16)
        cT = sb("cT", [P, 2, T], BF16)
        xnr = sb("xnr", [P, NT, D])
        xcr = sb("xcr", [P, NT, D], BF16)
        xr = sb("xr", [P, NT, D])
        s1 = sb("s1", [P, NT, D])
        x1 = sb("x1", [P, NT, D])
        x1b = sb("x1b", [P, NT, D])
        st2 = sb("st2", [P, NT, 6])
        mv2 = sb("mv2", [P, NT, 2])
        r3t = sb("r3t", [P, NT])
        r3 = sb("r3", [P, NT])
        h2 = sb("h2", [P, NT, D])
        h2T = sb("h2T", [P, T])
        hid = sb("hid", [P, NJ, T])
        sres = sb("sres", [P, NT, D])
        ga = sb("ga", [P, 2, T])
        warm = sb("warm", [P, NT])
        lin = sb("lin", [P, 2, T])
        gc = sb("gc", [P, 2, T])
        act_t = sb("act_t", [P, 3, T])
        cb = sb("cb", [P, NT, D], BF16)
        z = sb("z", [P, NT, D], BF16)
        zth = sb("zth", [P, NT, D])
        ob = sb("ob", [P, NT, D])

        blank_set = signal("blank_set", 1)
        va_set = signal("va_set", 1)
        stacks_set = signal("stacks_set", 1)
        ident_set = signal("ident_set", 1)
        masks_set = signal("masks_set", 1)
        weights_in = signal("weights_in", 1)
        experts_in = signal("experts_in", 1)
        later_weights_in = signal("later_weights_in", 1)
        expert_ps = signal("expert_ps", 1)
        expert_sb = signal("expert_sb", 1)
        consts = signal("consts", 1)
        x_in = signal("x_in", 16)
        xr_in = signal("xr_in", 16)
        xn_copied = signal("xn_copied", 16)
        xc_copied = signal("xc_copied", 16)
        stacks_in = signal("stacks_in", 16 * 6)
        qk_out = signal("qk_out", 16 * 6)
        nm_out = signal("nm_out", 16)
        shift_in = signal("shift_in", 16 * 2)
        out_st = signal("out_st", 16)
        stats_ok = signal("stats_ok", 2)
        mv_ok = signal("mv_ok", 1)
        r1_step = signal("r1_step", 2)
        r2_step = signal("r2_step", 4)
        xn_ok = signal("xn_ok", 2)
        xc_ok = signal("xc_ok", 1)
        sq_ok = signal("sq_ok", 2)
        rs_step = signal("rs_step", 2)
        h0_ok = signal("h0_ok", NT)
        nf_ok = signal("nf_ok", 2)
        hT_ps = signal("hT_ps", 1)
        hT_ok = signal("hT_ok", 1)
        q_ps = signal("q_ps", 1)
        k_ps = signal("k_ps", 1)
        v_ps = signal("v_ps", 1)
        u_ps = signal("u_ps", 1)
        g_ps = signal("g_ps", 1)
        qkhi_ok = signal("qkhi_ok", 2)
        qkr_ok = signal("qkr_ok", 2)
        qkmid_ok = signal("qkmid_ok", 2)
        qklo_ok = signal("qklo_ok", 2)
        v_ok = signal("v_ok", 1)
        st_ok = signal("st_ok", 1)
        gpre_ok = signal("gpre_ok", 1)
        gth_ok = signal("gth_ok", 1)
        s_ps = signal("s_ps", 2 * NCH)
        mx_ok = signal("mx_ok", 2 * NCH)
        nm_step = signal("nm_step", 4)
        nm_ps = signal("nm_ps", 1)
        nmT_ok = signal("nmT_ok", 1)
        sT_ps = signal("sT_ps", NCH)
        exp_ok = signal("exp_ok", NCH)
        pt_ok = signal("pt_ok", NCH)
        pv_ps = signal("pv_ps", NCH)
        ot_ok = signal("ot_ok", NG)
        ott_ps = signal("ott_ps", NG)
        rz_ok = signal("rz_ok", NG)
        ao_ok = signal("ao_ok", NG)
        aoT_ps = signal("aoT_ps", 1)
        aoT_ok = signal("aoT_ok", 1)
        wo_ps = signal("wo_ps", 1)
        cw_ps = signal("cw_ps", 1)
        t1_ok = signal("t1_ok", 1)
        s1_ok = signal("s1_ok", 1)
        x1_ok = signal("x1_ok", 1)
        x1b_ok = signal("x1b_ok", 1)
        st2_ok = signal("st2_ok", 1)
        mv2_ok = signal("mv2_ok", 1)
        r3_step = signal("r3_step", 2)
        h2_ok = signal("h2_ok", 1)
        h2T_ps = signal("h2T_ps", 1)
        h2T_ok = signal("h2T_ok", 1)
        w1_ps = signal("w1_ps", NJ)
        hid_ok = signal("hid_ok", NJ)
        w2_ps = signal("w2_ps", 1)
        s_ok = signal("s_ok", 1)
        nfT_ps = signal("nfT_ps", 1)
        nfn_ok = signal("nfn_ok", 1)
        nfT_ok = signal("nfT_ok", 1)
        lg_ps = signal("lg_ps", 1)
        lg_ok = signal("lg_ok", 1)
        route = signal("route", 13)
        ex_ok = signal("ex_ok", 1)
        cT_ps = signal("cT_ps", 1)
        cT_ok = signal("cT_ok", 1)
        up_ps = signal("up_ps", E)
        ga_ok = signal("ga_ok", E)
        lin_ok = signal("lin_ok", E)
        clip_ok = signal("clip_ok", E)
        gc_ok = signal("gc_ok", E)
        act_ok = signal("act_ok", E)
        down_ps = signal("down_ps", E)
        cb_ok = signal("cb_ok", 1)
        z_ok = signal("z_ok", 1)
        zth_ok = signal("zth_ok", 1)
        y_ok = signal("y_ok", 1)
        w_ok = signal("w_ok", 1)
        ob_ok = signal("ob_ok", 1)

        spare = {}

        def apart(eng, b):
            if not isinstance(b, int):
                eng.sem_inc(spare[eng], 1)

        def set_spare(eng, name):
            spare[eng] = ctx.enter_context(nc.semaphore(name))

        def done(signal, batch, count=None):
            value = batch * signal.per + (signal.per if count is None else count)
            if isinstance(value, int) and value <= 0:
                return blank_set.sem, 1
            return signal.sem, value

        x_d = a["x"].rearrange("b (t p) d -> b p t d", p=P)
        o_d = out.rearrange("b (t p) d -> b p t d", p=P)

        def row_of(v):
            return v.rearrange("(o d) -> o d", o=1).broadcast_to([P, v.shape[0]])

        def col_of(v, n=1):
            return v.rearrange("(j p) -> p j", j=n)

        WEIGHTS = [
            (wq[:], a["WQ"]), (wk[:], a["WK"]), (bw[:, 0:N], a["Bw"]), (wv[:], a["WV"]), (wg[:], a["Wg"]),
            *((cols[n][:], col_of(a[n])) for n in ("ln1_g", "ln1_b", "bQ", "bK")), (acol[0:N, :], col_of(a["A"])),
            (rows["bV"][:], row_of(a["bV"])), (rows["bg"][:], row_of(a["bg"])), (rows["nw"][:], row_of(a["norm_weight"])),
        ]
        LATER_WEIGHTS = [
            (gw[:], a["gate_weight"].rearrange("e h -> h e")), (gbias_b[:], row_of(a["gate_bias"])),
            (mb_b[:], a["mlp1_bias"].rearrange("e (i s) -> i e s", s=2)), (cw[0:N, :], a["Cw"]), (wo[:], a["WO"]),
            (ncw[N:N + 1, :], a["bO"].rearrange("(o d) -> o d", o=1)),
            *((b2st[E * c:E * (c + 1), :], a["mlp2_bias"]) for c in range(NPART)),
            (w1[:], a["W1"]), (w2[:], a["W2"].rearrange("(j p) d -> p j d", j=NJ)),
            *((cols[n][:], col_of(a[n])) for n in ("ln2_g", "ln2_b")),
            (b1c[:], col_of(a["b1"], NJ)), (rows["b2"][:], row_of(a["b2"])),
        ]
        EXPERTS = [
            (m1raw[:], a["mlp1_weight"].rearrange("e (i s) h -> i e s h", s=2)),
            (m2raw[:], a["mlp2_weight"].rearrange("e h i -> h e i")),
        ]
        BLANKS = [
            (half[:], -0.5), (ident[:], 0.0), (identb[:], 0.0), (bw[:, N:], 0.0), (cw[N:, :], 0.0), (ncw[:], 0.0), (b2st[:], 0.0),
            (mask[:], 0.0), (tie[:], 0.0), (sel[:], 0.0),
        ]
        two_ones = float(np.array([0x3F803F80], np.uint32).view(np.float32)[0])
        LATER_BLANKS = [
            (kd[0][:].rearrange("p n t -> p (n t)").bitcast(F32), two_ones), (zrow[:], 0.0), (cp[:], 0.0),
            (qz[0][:], 0.0), (st[:], 0.0),
        ]
        ONES = [(st[N:N + 1], 1.0), *((va[:, i, :, :, DH:DH + 1], 1.0) for i in range(2))]
        ALL_BLANKS = len(BLANKS) + len(LATER_BLANKS)
        N_MASKS = 3 + NPART

        qk_d = nc.dram_tensor("qk_parts", (2, P, 6, T), BF16, kind="Internal").ap()
        nm_d = nc.dram_tensor("minus_maxima", (NPART * H, T), BF16, kind="Internal").ap()

        def at(tensor, b):
            return tensor[b] if isinstance(b, int) else tensor[bass.ds(b, 1)].rearrange("o p t d -> (o p) t d")

        block = ctx.enter_context(nc.Block())

        def schedule(eng, body):
            for b in range(-2, 2):
                body(b, b % 2)
            with eng.Fori(1, B // 2 - 1) as pair:
                body(2 * pair, 0)
                body(2 * pair + 1, 1)
            for b in range(B - 2, B + 1):
                body(b, b % 2)

        def has(b):
            return not isinstance(b, int) or 0 <= b < B

        def all_set(eng):
            for s, n in ((blank_set, ALL_BLANKS + len(ONES)), (va_set, 1), (ident_set, 2), (weights_in, 16 * len(WEIGHTS)),
                         (later_weights_in, 16 * len(LATER_WEIGHTS)), (consts, CONSTS)):
                eng.wait_ge(s.sem, n)

        def start(b, which):
            return isinstance(b, int) and b == which

        @block.sync
        def _(sp):
            sp.dma_start(xl[:, 0], at(x_d, 0)).then_inc(x_in.sem, 16)
            for dst, src in WEIGHTS:
                sp.dma_start(dst, src).then_inc(weights_in.sem, 16)
            sp.wait_ge(*done(stats_ok, 0))
            sp.dma_start(xl[:, 1], at(x_d, 1)).then_inc(x_in.sem, 16)
            sp.wait_ge(blank_set.sem, len(BLANKS))
            for dst, src in LATER_WEIGHTS:
                sp.dma_start(dst, src, allow_slow_non_contiguous=True).then_inc(later_weights_in.sem, 16)

            def body(b, q):
                if has(b) and has(b + 2):
                    sp.wait_ge(*done(xn_ok, b))
                    sp.dma_start(xl[:, q], at(x_d, b + 2)).then_inc(x_in.sem, 16)
                if has(b - 1):
                    sp.wait_ge(*done(ob_ok, b - 1))
                    sp.dma_start(at(o_d, b - 1), ob[:]).then_inc(out_st.sem, 16)
                if has(b):
                    sp.dma_start(xr[:], at(x_d, b)).then_inc(xr_in.sem, 16)
                if start(b, -2):
                    all_set(sp)
                if has(b + 2):
                    sp.wait_ge(*done(stacks_in, b + 1))
                    for n, parts in enumerate((qp, kp)):
                        sp.wait_ge(*done(qklo_ok, b + 2, n + 1))
                        for first, count in ((0, 3), (3, 2), (5, 1)):
                            src = parts[:, 0:count] if n else \
                                parts[:, 3 - count:4 - count].to_broadcast([P, count, T])
                            sp.dma_start(qk_d[n, :, first:first + count], src).then_inc(qk_out.sem, 16)
                    if start(b, -1):
                        sp.wait_ge(stacks_set.sem, 2)
                    sp.wait_ge(*done(sT_ps, b))
                    sp.wait_ge(*done(qk_out, b + 2))
                    for par in range(2):
                        first = 64 * par
                        sp.dma_start(qz[q][first + SHIFT:first + SHIFT + NPART, :, par],
                                     zrow[:].unsqueeze(1).to_broadcast([NPART, NPAIR, T])).then_inc(stacks_in.sem, 16)
                        for n, dst in enumerate((qz[q][first:first + SHIFT, :, par], kd[q][first:first + SHIFT])):
                            src = qk_d[n].rearrange("(p two d) c t -> two (d c) p t", two=2, d=DH)[par]
                            sp.dma_start(dst, src).then_inc(stacks_in.sem, 16)
                if has(b + 1):
                    sp.wait_ge(*done(nmT_ok, b + 1))
                    sp.wait_ge(*done(shift_in, b))
                    sp.dma_start(nm_d, nmT[:]).then_inc(nm_out.sem, 16)
                    sp.wait_ge(*done(nm_out, b + 1))
                    for par in range(2):
                        sp.dma_start(qz[1 - q][64 * par + SHIFT:64 * par + SHIFT + NPART, :, par],
                                     nm_d.rearrange("(r p two) t -> two r p t", r=NPART, two=2)[par]).then_inc(shift_in.sem, 16)
                    sp.wait_ge(*done(xn_ok, b + 1))
                    sp.wait_ge(*done(x1_ok, b))
                    sp.dma_start(xnr[:], xn[:, 1 - q]).then_inc(xn_copied.sem, 16)
                    sp.wait_ge(*done(xc_ok, b + 1))
                    sp.wait_ge(*done(z_ok, b))
                    sp.dma_start(xcr[:], xc[:, 1 - q]).then_inc(xc_copied.sem, 16)

            schedule(sp, body)
            sp.wait_ge(*done(out_st, B - 1))

        @block.tensor
        def _(pe):
            pe.wait_ge(ident_set.sem, 2)
            pe.wait_ge(experts_in.sem, 16 * len(EXPERTS))
            for k in range(6):
                for c in range(4):
                    if k < 4:
                        src = m1raw[:, 2 * k + c // 2, c % 2, :]
                    else:
                        src = m2raw[:, 4 * (k - 4) + c, :]
                    mm = nc.tensor.transpose(bank_bf(k)[:, P * c:P * (c + 1)], src, identb[:])
                mm.then_inc(expert_ps.sem, 1)
            pe.wait_ge(weights_in.sem, 16 * len(WEIGHTS))

            def score_t(b, q, n):
                g, j = n // NT, n % NT
                if n == 0:
                    pe.wait_ge(*done(stacks_in, b))
                    pe.wait_ge(*done(shift_in, b))
                if n >= 2:
                    pe.wait_ge(*done(exp_ok, b, n - 1))
                else:
                    pe.wait_ge(*done(hid_ok, b - 1))
                    if isinstance(b, int) and b == 0:
                        for s in (st_ok, qkr_ok, v_ok):
                            pe.wait_ge(*done(s, b + 1))
                w_q = 2 * P if j < NT - 1 else P
                for pr in range(2):
                    p = 2 * g + pr
                    o = bank(2 * (n % 2) + pr).rearrange("p (r q) -> p r q", r=2)[:, :, 0:w_q]
                    mm = nc.tensor.matmul(o, kd[q][:, p, P * j:P * (j + 1)], qz[q][:, p, :, P * j:P * j + w_q],
                                          start=True, stop=True)
                mm.then_inc(sT_ps.sem, 1)

            def score(b, q, n, pr):
                g, i = n // NT, n % NT
                if n == 0:
                    pe.wait_ge(*done(stacks_in, b))
                    pe.wait_ge(*done(gc_ok, b - 2, E))
                    pe.wait_ge(*done(gpre_ok, b))
                else:
                    pe.wait_ge(*done(mx_ok, b, 2 * n - 1 + pr))
                lo = 0 if i else P
                o = bank(4 + pr).rearrange("p (r k) -> p r k", r=2)
                p = 2 * g + pr
                for par in range(2):
                    nc.tensor.matmul(o[:, par, lo:], qz[q][:, p, par, P * i:P * (i + 1)],
                                     kd[q][:, p, P * (i - 1) + lo:P * (i + 1)], start=par == 0, stop=False,
                                     skip_group_check=True)
                nc.tensor.matmul(o[:, :, lo:], identb[:], mask[:, :, lo:], start=False, stop=True,
                                 skip_group_check=True).then_inc(s_ps.sem, 1)

            def values(b, q, n):
                g, j = n // NT, n % NT
                pe.wait_ge(*done(pt_ok, b, n + 1))
                if n == 0:
                    pe.wait_ge(*done(v_ok, b))
                    pe.wait_ge(*done(s_ok, b - 1))
                    if isinstance(b, int) and b == 0:
                        pe.wait_ge(*done(lg_ok, b + 1))
                elif j == 0:
                    pe.wait_ge(*done(ot_ok, b, g))
                w_q = 2 * P if j < NT - 1 else P
                for c in range(HG):
                    mm = nc.tensor.matmul(ps[32 * c:32 * (c + 1), 6, P * j:P * j + w_q], va[:, q, j, HG * g + c, :],
                                          pt[:, n % NPT, c, 0:w_q], start=j == 0, stop=True,
                                          skip_group_check=True)
                mm.then_inc(pv_ps.sem, 1)

            def turn_out(b, g):
                pe.wait_ge(*done(ot_ok, b, g + 1))
                if g == 0:
                    pe.wait_ge(*done(cb_ok, b - 1))
                else:
                    pe.wait_ge(*done(ao_ok, b, g))
                for t in range(NT):
                    mm = nc.tensor.transpose(bank_t(7)[:, t], ot[:, P * t:P * (t + 1)], ident[:])
                mm.then_inc(ott_ps.sem, 1)

            def turn4(k, src):
                for t in range(NT):
                    mm = nc.tensor.transpose(k[:, P * t:P * (t + 1)], src(t), identb[:] if src(t).dtype == BF16 else ident[:])
                return mm

            def body(b, q):
                main, nxt, nx2 = has(b), has(b + 1), has(b + 2)

                def turn_h0():
                    pe.wait_ge(*done(h0_ok, b + 2))
                    if main:
                        pe.wait_ge(*done(exp_ok, b, NCH))
                    else:
                        for s in (st_ok, qkr_ok, v_ok):
                            pe.wait_ge(*done(s, b + 1))
                    turn4(bank(0), lambda t: h0[:, t]).then_inc(hT_ps.sem, 1)

                def project_qk():
                    pe.wait_ge(*done(hT_ok, b + 2))
                    nc.tensor.matmul(bank(1), wq[:], hT[:], start=True, stop=True).then_inc(q_ps.sem, 1)
                    nc.tensor.matmul(bank(2), wk[:], hT[:], start=True, stop=True).then_inc(k_ps.sem, 1)

                def project_uv():
                    nc.tensor.matmul(bank(0), bw[:], hT[:], start=True, stop=True).then_inc(u_ps.sem, 1)
                    for t in range(NT):
                        mm = nc.tensor.matmul(bank_t(3)[:, t], hT[:, P * t:P * (t + 1)], wv[:], start=True, stop=True)
                    mm.then_inc(v_ps.sem, 1)

                if start(b, -2):
                    pe.wait_ge(expert_sb.sem, 6)
                if nx2 and not main:
                    turn_h0()
                    project_qk()
                    project_uv()
                if start(b, -1):
                    all_set(pe)
                    pe.wait_ge(masks_set.sem, N_MASKS)
                for n in range(NCH + 4):
                    if main and n < NCH:
                        score_t(b, q, n)
                    if nxt and n < NCH:
                        score(b + 1, 1 - q, n, 0)
                    if main and 3 <= n < NCH + 3:
                        values(b, q, n - 3)
                    if nxt and n < NCH:
                        score(b + 1, 1 - q, n, 1)
                    if main and n >= 7 and (n - 7) % NT == 0 and n < NCH + 3:
                        turn_out(b, (n - 7) // NT)
                    if nx2 and main and n == NCH:
                        turn_h0()
                    if nx2 and main and n == NCH + 2:
                        project_qk()
                if main:
                    turn_out(b, NG - 1)
                if nx2 and main:
                    project_uv()
                if nxt:
                    pe.wait_ge(*done(nm_step, b + 1))
                    apart(pe, b)
                    for t in range(NT):
                        mm = nc.tensor.transpose(bank_bf(5)[0:NPART * H, P * t:P * (t + 1)], nm[:, t].rearrange("p r h -> p (r h)"), identb[:])
                    mm.then_inc(nm_ps.sem, 1)
                    pe.wait_ge(*done(route, b + 1))
                    turn4(bank_bf(5, 1), lambda t: cp[:, t]).then_inc(cT_ps.sem, 1)
                if main:
                    pe.wait_ge(*done(st_ok, b))
                    for t in range(NT):
                        nc.tensor.matmul(bank_t(4)[:, t], st[:, q, P * t:P * (t + 1)], cw[:], start=True, stop=True)
                    for t in range(NT):
                        mm = nc.tensor.matmul(bank_t(6)[:, t], st[:, q, P * t:P * (t + 1)], ncw[:], start=t == 0, stop=False,
                                              skip_group_check=True)
                    mm.then_inc(cw_ps.sem, 1)
                    pe.wait_ge(*done(ao_ok, b, NG))
                    turn4(bank(7), lambda t: ao[:, t]).then_inc(aoT_ps.sem, 1)

                if nx2:
                    for s in ((nmT_ok, cT_ok) if nxt else ()):
                        pe.wait_ge(*done(s, b + 1))
                    if not main:
                        pe.wait_ge(*done(gpre_ok, b + 1))
                    for t in range(NT):
                        mm = nc.tensor.matmul(bank_t(5)[:, t], hT[:, P * t:P * (t + 1)], wg[:], start=True, stop=True)
                    mm.then_inc(g_ps.sem, 1)
                def up(e):
                    k = 3 * (e % 2)
                    if e < 2 and nx2:
                        for s in ((st_ok, qkr_ok), (v_ok, gpre_ok))[e]:
                            pe.wait_ge(*done(s, b + 2))
                    if e == 1:
                        pe.wait_ge(*done(s1_ok, b))
                    elif e >= 2:
                        pe.wait_ge(*done(ga_ok, b, e - 1))
                        pe.wait_ge(*done(gc_ok, b, e - 1))
                    for s in range(2):
                        nc.tensor.matmul(bank(k + s), m1[:, e, s], nfT[:, q], start=True, stop=True)
                    nc.tensor.matmul(bank(k + 2), sel[:, e], cT[:, q], start=True, stop=True).then_inc(up_ps.sem, 1)

                def down(e):
                    pe.wait_ge(*done(act_ok, b, e + 1))
                    for t in range(NT):
                        mm = nc.tensor.matmul(bank_t(7)[:, t], act_t[:, e % 3, P * t:P * (t + 1)], m2[:, e], start=False,
                                              stop=e == E - 1, skip_group_check=True)
                    mm.then_inc(down_ps.sem, 1)

                def turn_nf():
                    turn4(bank_bf(6), lambda t: nf[:, t]).then_inc(nfT_ps.sem, 1)

                def logits():
                    pe.wait_ge(*done(nfn_ok, b + 2))
                    for t in range(NT):
                        mm = nc.tensor.matmul(bank(6)[:, T // 2 + E * t:T // 2 + E * (t + 1)], nfn[:, P * t:P * (t + 1)], gw[:], start=True, stop=True)
                    mm.then_inc(lg_ps.sem, 1)

                def mlp_up(j):
                    if j == 0:
                        pe.wait_ge(*done(h2T_ok, b))
                    elif j == 1:
                        pe.wait_ge(*done(ga_ok, b, E - 1))
                    elif j == 3:
                        pe.wait_ge(*done(gc_ok, b, E - 1))
                    nc.tensor.matmul(bank((6, 0, 1, 2)[j]), w1[:, P * j:P * (j + 1)], h2T[:], start=True, stop=True).then_inc(w1_ps.sem, 1)

                if main:
                    pe.wait_ge(*done(nfT_ok, b))
                    up(0)
                    pe.wait_ge(*done(aoT_ok, b))
                    for t in range(NT):
                        mm = nc.tensor.matmul(bank_t(6)[:, t], aoT[:, P * t:P * (t + 1)], wo[:], start=False, stop=True,
                                              skip_group_check=True)
                    mm.then_inc(wo_ps.sem, 1)
                    up(1)
                    for t in range(NT):
                        nc.tensor.matmul(bank_t(7)[:, t], cT[:, q, P * t:P * (t + 1)], b2st[:], start=t == 0,
                                         stop=False, skip_group_check=True)
                    for e in range(2, E):
                        up(e)
                        if nx2 and e == 3:
                            pe.wait_ge(*done(nf_ok, b + 2))
                            pe.wait_ge(*done(t1_ok, b))
                            turn_nf()
                        if nx2 and e == 4:
                            logits()
                        down(e - 2)
                        if e == 6:
                            pe.wait_ge(*done(h2_ok, b))
                            if nx2:
                                pe.wait_ge(*done(lg_ok, b + 2))
                            turn4(bank(6), lambda t: h2[:, t]).then_inc(h2T_ps.sem, 1)
                    mlp_up(0)
                    mlp_up(1)
                    mlp_up(2)
                    down(E - 2)
                    mlp_up(3)
                    down(E - 1)
                    for t in range(NT):
                        for j in range(NJ):
                            if t == 0:
                                pe.wait_ge(*done(hid_ok, b, j + 1))
                            mm = nc.tensor.matmul(bank_t(6)[:, t], hid[:, j, P * t:P * (t + 1)], w2[:, j], start=j == 0, stop=j == NJ - 1)
                    mm.then_inc(w2_ps.sem, 1)
                elif nx2:
                    pe.wait_ge(later_weights_in.sem, 16 * len(LATER_WEIGHTS))
                    pe.wait_ge(*done(nf_ok, b + 2))
                    pe.wait_ge(*done(lg_ok, b + 1))
                    turn_nf()
                    logits()

            set_spare(pe, "pe_waited")
            schedule(pe, body)

        @block.scalar
        def _(act):
            for dst, src in EXPERTS:
                act.dma_start(dst, src).then_inc(experts_in.sem, 16)
            for k in range(6):
                act.wait_ge(expert_ps.sem, k + 1)
                dst = m1[:, 2 * k:2 * k + 2].rearrange("p e s i -> p (e s i)") if k < 4 else \
                    m2[:, 4 * (k - 4):4 * (k - 3)].rearrange("p e d -> p (e d)")
                nc.scalar.activation(dst, bank_bf(k), ACT.Copy).then_inc(expert_sb.sem, 1)
            def body(b, q):
                main, nxt, nx2 = has(b), has(b + 1), has(b + 2)
                if has(b - 1):
                    act.wait_ge(*done(z_ok, b - 1))
                    act.wait_ge(*done(w_ok, b - 2))
                    nc.scalar.activation(zth[:], z[:], ACT.Tanh, scale=0.5).then_inc(zth_ok.sem, 1)
                if start(b, -1):
                    all_set(act)
                if nxt:
                    act.wait_ge(*done(gpre_ok, b + 1))
                    act.wait_ge(*done(x1_ok, b - 1))
                    nc.scalar.activation(gth[:, 1 - q], gpre[:], ACT.Tanh, scale=0.5).then_inc(gth_ok.sem, 1)

                def cast_x():
                    act.wait_ge(*done(xn_ok, b + 2))
                    act.wait_ge(*done(xc_copied, b))
                    nc.scalar.activation(xc[:, q], xn[:, q], ACT.Copy).then_inc(xc_ok.sem, 1)

                def norm_h(t):
                    act.wait_ge(*done(r2_step, b + 2))
                    act.wait_ge(*done(hT_ps, b + 1))
                    nc.scalar.activation(h0[:, t], xn[:, q, t], ACT.Copy, scale=r2[:, t:t + 1]).then_inc(h0_ok.sem, 1)

                def hT_in():
                    act.wait_ge(*done(hT_ps, b + 2))
                    act.wait_ge(*done(g_ps, b + 1))
                    nc.scalar.activation(hT[:], bank(0), ACT.Identity, bias=cols["ln1_b"][:], scale=cols["ln1_g"][:]).then_inc(hT_ok.sem, 1)

                def qk_in():
                    act.wait_ge(*done(qk_out, b + 1))
                    for n, (signal_ps, dst, bias) in enumerate(((q_ps, qp, "bQ"), (k_ps, kp, "bK"))):
                        act.wait_ge(*done(signal_ps, b + 2))
                        nc.scalar.activation(dst[:, 0], bank(1 + n), ACT.Identity, bias=cols[bias][:]).then_inc(qkhi_ok.sem, 1)

                if nx2 and not main:
                    cast_x()
                    for t in range(NT):
                        norm_h(t)
                    if start(b, -2):
                        act.wait_ge(weights_in.sem, 16 * len(WEIGHTS))
                    hT_in()
                    qk_in()
                if main:
                    nc.scalar.activation(warm[:], half[:], ACT.Exp)
                for n in range(NCH + 4):
                    if main and n < NCH:
                        act.wait_ge(*done(sT_ps, b, n + 1))
                        if n >= NPT:
                            act.wait_ge(*done(pv_ps, b, n - NPT + 1))
                        else:
                            act.wait_ge(*done(pv_ps, b - 1, NCH - NPT + n + 1))
                        w_q = 2 * P if n % NT < NT - 1 else P
                        src = ps[:, 2 * (n % 2):2 * (n % 2) + 2, :].rearrange("p c (r q) -> p (c r) q", r=2)[:, :, 0:w_q]
                        nc.scalar.activation(pt[:, n % NPT, :, 0:w_q], src, ACT.Exp, scale=SCALE).then_inc(exp_ok.sem, 1)
                    if main and n >= 6 and (n - 6) % NT == 0:
                        g = (n - 6) // NT
                        act.wait_ge(*done(pv_ps, b, NT * (g + 1)))
                        act.wait_ge(*done(ott_ps, b, g))
                        nc.scalar.activation(ot[:], bank(6), ACT.Copy).then_inc(ot_ok.sem, 1)
                    if nx2 and main and n == 7:
                        cast_x()
                    if nx2 and main and 10 <= n < 10 + NT:
                        norm_h(n - 10)
                    if nxt and n == 1:
                        act.wait_ge(*done(route, b + 1, 4))
                        nc.scalar.activation(ex[:], ld[:], ACT.Exp).then_inc(ex_ok.sem, 1)
                    if nx2 and main and n == NCH:
                        hT_in()
                    if main and n == NCH:
                        nc.scalar.activation(warm[:], half[:], ACT.Gelu_apprx_sigmoid)
                if nx2 and main:
                    qk_in()
                if nxt:
                    act.wait_ge(*done(nm_ps, b + 1))
                    act.wait_ge(*done(cT_ps, b + 1))
                    act.wait_ge(*done(shift_in, b))
                    nc.scalar.activation(nmT[:], bank_bf(5)[0:NPART * H, :], ACT.Copy).then_inc(nmT_ok.sem, 1)
                    act.wait_ge(*done(down_ps, b - 1))
                    nc.scalar.activation(cT[:, 1 - q], bank_bf(5, 1), ACT.Copy).then_inc(cT_ok.sem, 1)
                def nfn_in():
                    act.wait_ge(*done(nfT_ps, b + 2))
                    act.wait_ge(*done(nfT_ok, b + 1))
                    act.wait_ge(*done(lg_ps, b + 1))
                    nc.scalar.activation(nfn[:], bank_bf(6), ACT.Copy).then_inc(nfn_ok.sem, 1)

                if main:
                    act.wait_ge(*done(aoT_ps, b))
                    act.wait_ge(*done(wo_ps, b - 1))
                    nc.scalar.activation(aoT[:], bank(7), ACT.Copy).then_inc(aoT_ok.sem, 1)
                    for e in range(E):
                        act.wait_ge(*done(up_ps, b, e + 1))
                        if e >= 2:
                            act.wait_ge(*done(gc_ok, b, e - 1))
                        else:
                            act.wait_ge(*done(gc_ok, b - 1))
                        act.wait_ge(*(done(act_ok, b, e - 1) if e >= 2 else done(act_ok, b - 1)))
                        nc.scalar.activation(lin[:, e % 2], bank(3 * (e % 2) + 1), ACT.Identity, bias=mbias[:, e, 1:2]).then_inc(lin_ok.sem, 1)
                        nc.scalar.activation(ga[:, e % 2], bank(3 * (e % 2)), ACT.Gelu_apprx_sigmoid, bias=mbias[:, e, 0:1]).then_inc(ga_ok.sem, 1)
                        if nx2 and e == 3:
                            nfn_in()
                        if e == 6:
                            act.wait_ge(*done(h2T_ps, b))
                            act.wait_ge(*done(w1_ps, b - 1))
                            nc.scalar.activation(h2T[:], bank(6), ACT.Identity, bias=cols["ln2_b"][:], scale=cols["ln2_g"][:]).then_inc(h2T_ok.sem, 1)
                    for j, k in enumerate((6, 0, 1, 2)):
                        act.wait_ge(*done(w1_ps, b, j + 1))
                        if j == 0:
                            act.wait_ge(*done(w2_ps, b - 1))
                        nc.scalar.activation(hid[:, j], bank(k), ACT.Gelu, bias=b1c[:, j:j + 1]).then_inc(hid_ok.sem, 1)
                    act.wait_ge(*done(down_ps, b))
                    act.wait_ge(*done(z_ok, b - 1))
                    nc.scalar.activation(cb[:], bank_t(7), ACT.Copy).then_inc(cb_ok.sem, 1)
                elif nx2:
                    nfn_in()

            schedule(act, body)

        @block.vector
        def _(dve):
            def finish(b, part):
                if part == 0:
                    dve.wait_ge(*done(zth_ok, b))
                    nc.vector.scalar_tensor_tensor(out=zth[:], in0=zth[:], scalar=1.0, in1=z[:], op0=ALU.add, op1=ALU.mult).then_inc(y_ok.sem, 1)
                else:
                    dve.wait_ge(*done(y_ok, b))
                    dve.wait_ge(*done(s_ok, b))
                    nc.vector.scalar_tensor_tensor(out=sres[:], in0=zth[:], scalar=0.5, in1=sres[:], op0=ALU.mult, op1=ALU.mult).then_inc(w_ok.sem, 1)

            def norm_stats(b, q, tiles):
                if tiles[0] == 0:
                    dve.wait_ge(*done(x_in, b))
                    dve.wait_ge(*done(mv_ok, b - 1))
                for t in tiles:
                    bn = nc.vector.bn_stats(stats[:, t], xl[:, q, t])
                bn.then_inc(stats_ok.sem, 1)

            def norm_moments(b):
                dve.wait_ge(*done(stats_ok, b))
                dve.wait_ge(*done(xn_ok, b - 1))
                dve.wait_ge(*done(r2_step, b - 1, 1))
                apart(dve, b)
                for t in range(NT):
                    bn = nc.vector.bn_aggr(mv[:, t], stats[:, t])
                bn.then_inc(mv_ok.sem, 1)

            def norm_x(b, q, tiles):
                if tiles[0] == 0:
                    dve.wait_ge(*done(r1_step, b))
                    dve.wait_ge(*done(xn_copied, b - 2))
                for t in tiles:
                    ts = nc.vector.tensor_scalar(xn[:, q, t], xl[:, q, t], mv[:, t, 0:1], r1[:, t:t + 1], ALU.subtract, ALU.mult)
                ts.then_inc(xn_ok.sem, 1)

            def squares(b, q, tiles):
                if tiles[0] == 0:
                    dve.wait_ge(*done(xc_ok, b))
                    dve.wait_ge(*done(rs_step, b - 1))
                for t in tiles:
                    tr = nc.vector.tensor_tensor_reduce(junk[:, t], xc[:, q, t], xc[:, q, t], 1.0, 0.0, ALU.mult, ALU.add, sq[:, t:t + 1])
                tr.then_inc(sq_ok.sem, 1)

            def norm_f(b, q, tiles):
                if tiles[0] == 0:
                    dve.wait_ge(*done(rs_step, b))
                    dve.wait_ge(*done(nfT_ps, b - 1))
                for t in tiles:
                    ts = nc.vector.scalar_tensor_tensor(out=nf[:, t], in0=xc[:, q, t], scalar=rs[:, t:t + 1], in1=rows["nw"][:],
                                                        op0=ALU.mult, op1=ALU.mult)
                ts.then_inc(nf_ok.sem, 1)

            def route_rank(b):
                dve.wait_ge(*done(lg_ok, b))
                shape = [P, NT, E, E]
                nc.vector.tensor_tensor(dl[:], lg[:].unsqueeze(2).to_broadcast(shape), lg[:].unsqueeze(3).to_broadcast(shape),
                                        ALU.subtract).then_inc(route.sem, 1)
                nc.vector.tensor_reduce(lmax[:], lg[:], AX.X, ALU.max).then_inc(route.sem, 1)
                dve.wait_ge(*done(route, b, 2))
                nc.vector.tensor_tensor(bt[:], dl[:], tie[:].unsqueeze(1).to_broadcast(shape), ALU.is_gt).then_inc(route.sem, 1)
                nc.vector.tensor_tensor(ld[:], lg[:], lmax[:].unsqueeze(2).to_broadcast([P, NT, E]), ALU.subtract).then_inc(route.sem, 1)
                dve.wait_ge(*done(route, b, 4))
                nc.vector.tensor_reduce(rank[:], bt[:], AX.X, ALU.add).then_inc(route.sem, 1)

            def route_mix(b, part):
                if part == 0:
                    dve.wait_ge(*done(route, b, 5))
                    dve.wait_ge(*done(ex_ok, b))
                    nc.vector.scalar_tensor_tensor(out=exs[:], in0=rank[:], scalar=2.0, in1=ex[:], op0=ALU.is_lt, op1=ALU.mult).then_inc(route.sem, 1)
                    dve.wait_ge(*done(route, b, 6))
                    nc.vector.tensor_reduce(zs[:], exs[:], AX.X, ALU.add).then_inc(route.sem, 1)
                elif part == 1:
                    dve.wait_ge(*done(route, b, 7))
                    nc.vector.reciprocal(zr[:], zs[:]).then_inc(route.sem, 1)
                    dve.wait_ge(*done(route, b, 8))
                    nc.vector.tensor_tensor(cmb[:], exs[:], zr[:].unsqueeze(2).to_broadcast([P, NT, E]), ALU.mult).then_inc(route.sem, 1)
                elif part == 2:
                    dve.wait_ge(*done(route, b, 9))
                    dve.wait_ge(*done(cT_ps, b - 1))
                    nc.vector.tensor_copy(cp[:, :, 0:E], cmb[:]).then_inc(route.sem, 1)
                    dve.wait_ge(*done(route, b, 10))
                    nc.vector.tensor_tensor(cr[:], cmb[:], cp[:, :, 0:E], ALU.subtract).then_inc(route.sem, 1)
                else:
                    dve.wait_ge(*done(route, b, 11))
                    nc.vector.tensor_copy(cp[:, :, E:2 * E], cr[:]).then_inc(route.sem, 1)
                    dve.wait_ge(*done(route, b, 12))
                    nc.vector.tensor_tensor(cp[:, :, 2 * E:3 * E], cr[:], cp[:, :, E:2 * E], ALU.subtract).then_inc(route.sem, 1)

            for dst, value in BLANKS:
                nc.vector.memset(dst, value).then_inc(blank_set.sem, 1)
            norm_stats(0, 0, (0, 1))
            norm_stats(0, 0, (2, 3))
            norm_moments(0)
            for n, (dst, value) in enumerate(LATER_BLANKS):
                nc.vector.memset(dst, value).then_inc(blank_set.sem, 1)
                if n == 2:
                    norm_x(0, 0, (0, 1))
                    norm_x(0, 0, (2, 3))

            def later_setup():
                dve.wait_ge(blank_set.sem, ALL_BLANKS)
                dve.wait_ge(va_set.sem, 1)
                for dst, value in ONES:
                    nc.vector.memset(dst, value).then_inc(blank_set.sem, 1)
                dve.wait_ge(later_weights_in.sem, 16 * len(LATER_WEIGHTS))
                nc.vector.tensor_scalar(ncw[0:N, :], cw[0:N, :], -1.0, None, ALU.mult).then_inc(consts.sem, 1)
                nc.vector.tensor_copy(mbias[:, :, 0:1], mb_b[:, :, 0:1]).then_inc(consts.sem, 1)
                nc.vector.tensor_scalar(mbias[:, :, 1:2], mb_b[:, :, 1:2], 1.0, None, ALU.add).then_inc(consts.sem, 1)
                nc.vector.tensor_copy(gbias[:], gbias_b[:]).then_inc(consts.sem, 1)
                all_set(dve)

            def body(b, q):
                main, nxt, nx2 = has(b), has(b + 1), has(b + 2)

                def logits_in():
                    dve.wait_ge(*done(lg_ps, b + 2))
                    dve.wait_ge(*done(route, b + 1))
                    nc.vector.tensor_tensor(lg[:], bank(6)[:, T // 2:T // 2 + NT * E].rearrange("p (t e) -> p t e", e=E),
                                            gbias[:].unsqueeze(1).to_broadcast([P, NT, E]), ALU.add).then_inc(lg_ok.sem, 1)

                def qk_rest():
                    for n, (hi, rest, bias) in enumerate(((qp, qr, "bQ"), (kp, kr, "bK"))):
                        dve.wait_ge(*done(qkhi_ok, b + 2, n + 1))
                        dve.wait_ge(*done(qklo_ok, b + 1, n + 1))
                        nc.vector.scalar_tensor_tensor(out=rest[:], in0=bank(1 + n), scalar=cols[bias][:], in1=hi[:, 0],
                                                       op0=ALU.add, op1=ALU.subtract).then_inc(qkr_ok.sem, 1)

                def v_in():
                    dve.wait_ge(*done(v_ps, b + 2))
                    dve.wait_ge(*done(pv_ps, b))
                    shape = [P, NT, H, DH]
                    nc.vector.tensor_tensor(va[:, q, :, :, 0:DH], bank_t(3).rearrange("p t (h v) -> p t h v", v=DH),
                                            rows["bV"][:].rearrange("p (h v) -> p h v", v=DH).unsqueeze(1).to_broadcast(shape), ALU.add).then_inc(v_ok.sem, 1)

                def recur():
                    dve.wait_ge(*done(u_ps, b + 2))
                    dve.wait_ge(*done(cw_ps, b))
                    nc.vector.tensor_tensor_scan(st[0:N, q], acol[0:N, :].to_broadcast([N, T]), bank(0)[0:N], 0.0, ALU.mult, ALU.add).then_inc(st_ok.sem, 1)

                if nx2 and not main:
                    if start(b, -1):
                        norm_x(b + 2, q, (0, 1))
                        norm_x(b + 2, q, (2, 3))
                    squares(b + 2, q, (0, 1))
                    squares(b + 2, q, (2, 3))
                    if start(b, -2):
                        norm_stats(1, 1, (0, 1))
                        norm_stats(1, 1, (2, 3))
                        norm_moments(1)
                        dve.wait_ge(weights_in.sem, 16 * len(WEIGHTS))
                    norm_f(b + 2, q, (0, 1))
                    norm_f(b + 2, q, (2, 3))
                    if start(b, -2):
                        later_setup()
                    else:
                        dve.wait_ge(masks_set.sem, N_MASKS)
                        route_rank(0)
                    qk_rest()
                    recur()
                    v_in()
                for n in range(NCH + 5):
                    g, i = n // NT, n % NT
                    for pr in range(2):
                        step = 2 * n + pr
                        if nxt and n < NCH:
                            lo = 0 if i else P
                            dve.wait_ge(*done(s_ps, b + 1, step + 1))
                            if n == 0:
                                dve.wait_ge(*done(nm_step, b))
                            src = bank(4 + pr).rearrange("p (r k) -> p r k", r=2)[:, :, lo:]
                            h = HG * g + 2 * pr
                            nc.vector.tensor_reduce(mx[:, i, h:h + 2], src, AX.X, ALU.max).then_inc(mx_ok.sem, 1)
                        if has(b - 1) and step in (1, 3):
                            finish(b - 1, step // 2)
                        if nx2 and main:
                            if step in (5, 6):
                                norm_stats(b + 2, q, (0, 1) if step == 5 else (2, 3))
                            if step == 7:
                                norm_moments(b + 2)
                            if step in (12, 13):
                                norm_x(b + 2, q, (0, 1) if step == 12 else (2, 3))
                            if step in (18, 19):
                                squares(b + 2, q, (0, 1) if step == 18 else (2, 3))
                            if step in (27, 29):
                                norm_f(b + 2, q, (0, 1) if step == 27 else (2, 3))
                        if nxt and step in (9, 11, 15, 16):
                            route_mix(b + 1, (9, 11, 15, 16).index(step))
                    if nxt and n == NCH:
                        dve.wait_ge(*done(mx_ok, b + 1))
                        dve.wait_ge(*done(nm_ps, b))
                        nc.vector.tensor_scalar(nm[:, :, 0], mx[:], -1.0, None, ALU.mult).then_inc(nm_step.sem, 1)
                        dve.wait_ge(*done(nm_step, b + 1, 1))
                        nc.vector.scalar_tensor_tensor(out=mr[:], in0=mx[:], scalar=-1.0, in1=nm[:, :, 0], op0=ALU.mult, op1=ALU.subtract).then_inc(nm_step.sem, 1)
                        dve.wait_ge(*done(nm_step, b + 1, 2))
                        nc.vector.tensor_copy(nm[:, :, 1], mr[:]).then_inc(nm_step.sem, 1)
                        dve.wait_ge(*done(nm_step, b + 1, 3))
                        nc.vector.tensor_tensor(nm[:, :, 2], mr[:], nm[:, :, 1], ALU.subtract).then_inc(nm_step.sem, 1)
                    if main and n >= 8 and (n - 8) % NT == 0:
                        g = (n - 8) // NT
                        dve.wait_ge(*done(ott_ps, b, g + 1))
                        if g == 0:
                            dve.wait_ge(*done(aoT_ps, b - 1))
                        o = bank_t(7).rearrange("p t (h v) -> p t h v", v=VW)
                        dve.wait_ge(*done(ao_ok, b, g))
                        nc.vector.reciprocal(rz[:], o[:, :, :, DH]).then_inc(rz_ok.sem, 1)
                        dve.wait_ge(*done(rz_ok, b, g + 1))
                        nc.vector.tensor_tensor(ao[:, :, HG * DH * g:HG * DH * (g + 1)].rearrange("p t (h v) -> p t h v", v=DH),
                                                o[:, :, :, 0:DH], rz[:].unsqueeze(3).to_broadcast([P, NT, HG, DH]), ALU.mult).then_inc(ao_ok.sem, 1)
                if nx2 and main:
                    qk_rest()
                    v_in()
                if nx2 and main:
                    recur()
                if main:
                    dve.wait_ge(*done(cw_ps, b))
                    dve.wait_ge(*done(xn_copied, b))
                    nc.vector.tensor_tensor(s1[:], bank_t(4), xnr[:], ALU.add).then_inc(s1_ok.sem, 1)

                if nx2:
                    dve.wait_ge(*done(g_ps, b + 2))
                    dve.wait_ge(*done(gth_ok, b + 1))
                    nc.vector.tensor_tensor(gpre[:], bank_t(5), rows["bg"][:].unsqueeze(1).to_broadcast([P, NT, D]), ALU.add).then_inc(gpre_ok.sem, 1)
                if main:
                    def clip(e):
                        dve.wait_ge(*done(lin_ok, b, e + 1))
                        nc.vector.tensor_scalar(lin[:, e % 2], lin[:, e % 2], 1.0 - LIMIT, 1.0 + LIMIT, ALU.max, ALU.min).then_inc(clip_ok.sem, 1)

                    def gate(e):
                        dve.wait_ge(*done(ga_ok, b, e + 1))
                        dve.wait_ge(*(done(act_ok, b, e - 1) if e >= 2 else done(act_ok, b - 1)))
                        nc.vector.scalar_tensor_tensor(out=gc[:, e % 2], in0=ga[:, e % 2], scalar=G_LIMIT, in1=bank(3 * (e % 2) + 2),
                                                       op0=ALU.min, op1=ALU.mult).then_inc(gc_ok.sem, 1)

                    clip(0)
                    for e in range(E):
                        gate(e)
                        if e == 0:
                            dve.wait_ge(*done(wo_ps, b))
                            dve.wait_ge(*done(gth_ok, b))
                            dve.wait_ge(*done(x1b_ok, b - 1))
                            dve.wait_ge(*done(h2_ok, b - 1))
                            nc.vector.scalar_tensor_tensor(out=x1[:], in0=gth[:, q], scalar=1.0, in1=bank_t(6), op0=ALU.add, op1=ALU.mult).then_inc(t1_ok.sem, 1)
                        if e == 1:
                            dve.wait_ge(*done(x1_ok, b))
                            for t in range(NT):
                                bn = nc.vector.bn_stats(st2[:, t], x1[:, t])
                            bn.then_inc(st2_ok.sem, 1)
                        dve.wait_ge(*done(gc_ok, b, e + 1))
                        dve.wait_ge(*(done(down_ps, b, e - 2) if e >= 3 else done(down_ps, b - 1)))
                        dve.wait_ge(*done(clip_ok, b, e + 1))
                        nc.vector.tensor_tensor(act_t[:, e % 3], lin[:, e % 2], gc[:, e % 2], ALU.mult).then_inc(act_ok.sem, 1)
                        if e < E - 1:
                            clip(e + 1)
                        if e == 0:
                            dve.wait_ge(*done(t1_ok, b))
                            dve.wait_ge(*done(s1_ok, b))
                            nc.vector.scalar_tensor_tensor(out=x1[:], in0=x1[:], scalar=0.5, in1=s1[:], op0=ALU.mult, op1=ALU.add).then_inc(x1_ok.sem, 1)
                        if e == 1:
                            dve.wait_ge(*done(st2_ok, b))
                            apart(dve, b)
                            for t in range(NT):
                                bn = nc.vector.bn_aggr(mv2[:, t], st2[:, t])
                            bn.then_inc(mv2_ok.sem, 1)
                        if nx2 and e == 4:
                            logits_in()
                elif nx2:
                    logits_in()
                if nx2:
                    dve.wait_ge(*done(nfn_ok, b + 2))
                    nc.vector.tensor_copy(nfT[:, q], nfn[:]).then_inc(nfT_ok.sem, 1)
                    if not start(b, -2):
                        route_rank(b + 2)
                if main:
                    dve.wait_ge(*done(cb_ok, b))
                    dve.wait_ge(*done(xc_copied, b))
                    nc.vector.tensor_tensor(z[:], xcr[:], cb[:], ALU.add).then_inc(z_ok.sem, 1)
                if main:
                    dve.wait_ge(*done(w2_ps, b))
                    dve.wait_ge(*done(x1b_ok, b))
                    dve.wait_ge(*done(ob_ok, b - 1))
                    nc.vector.tensor_tensor(sres[:], bank_t(6), x1b[:], ALU.add).then_inc(s_ok.sem, 1)

            set_spare(dve, "dve_waited")
            schedule(dve, body)

        @block.gpsimd
        def _(pool):
            pool.wait_ge(blank_set.sem, len(BLANKS))
            for m in (ident, identb):
                nc.gpsimd.affine_select(out=m[:], in_=m[:], compare_op=ALU.not_equal, fill=1.0, base=0, pattern=[[-1, P]],
                                        channel_multiplier=1).then_inc(ident_set.sem, 1)

            def masks():
                nc.gpsimd.affine_select(out=mask[:, :, 0:P], in_=mask[:, :, 0:P], compare_op=ALU.is_ge, fill=NEG, base=-1, pattern=[[0, 2], [1, P]],
                                        channel_multiplier=-1).then_inc(masks_set.sem, 1)
                nc.gpsimd.affine_select(out=mask[:, :, P:], in_=mask[:, :, P:], compare_op=ALU.is_ge, fill=NEG, base=0, pattern=[[0, 2], [-1, P]],
                                        channel_multiplier=1).then_inc(masks_set.sem, 1)
                nc.gpsimd.affine_select(out=tie[:], in_=tie[:], compare_op=ALU.is_ge, fill=TIE, base=0, pattern=[[-1, E], [1, E]],
                                        channel_multiplier=0).then_inc(masks_set.sem, 1)
                for c in range(NPART):
                    if c:
                        pool.wait_ge(masks_set.sem, 3 + c)
                    nc.gpsimd.affine_select(out=sel[:], in_=sel[:], compare_op=ALU.not_equal, fill=1.0, base=-E * c, pattern=[[-1, E], [0, P]],
                                            channel_multiplier=1).then_inc(masks_set.sem, 1)

            def inv_root(dst, tmp, src, scale, step, b, first, free):
                for s, sb_, c in free:
                    pool.wait_ge(*done(s, sb_, c))
                apart(pool, b)
                nc.gpsimd.tensor_scalar(tmp, src, scale, EPS, ALU.mult, ALU.add).then_inc(step.sem, 1)
                pool.wait_ge(*done(step, b, first + 1))
                nc.gpsimd.tensor_tensor(dst, tmp, half[:], ALU.pow).then_inc(step.sem, 1)

            def body(b, q):
                main, nxt, nx2 = has(b), has(b + 1), has(b + 2)
                for n in range(NCH + 1):
                    if main and n < NCH:
                        s = n % NPT
                        pool.wait_ge(*done(exp_ok, b, n + 1))
                        apart(pool, b)
                        sel1 = nc.gpsimd.affine_select(out=pt[:, s, :, 0:P], in_=pt[:, s, :, 0:P], compare_op=ALU.is_ge, fill=0.0, base=0,
                                                       pattern=[[0, HG], [1, P]], channel_multiplier=-1)
                        if n % NT < NT - 1:
                            sel1 = nc.gpsimd.affine_select(out=pt[:, s, :, P:], in_=pt[:, s, :, P:], compare_op=ALU.is_ge, fill=0.0, base=-1,
                                                           pattern=[[0, HG], [-1, P]], channel_multiplier=1)
                        sel1.then_inc(pt_ok.sem, 1)
                    if n == 2 and has(b - 1):
                        pool.wait_ge(*done(w_ok, b - 1))
                        pool.wait_ge(*done(xr_in, b - 1))
                        pool.wait_ge(*done(out_st, b - 2))
                        nc.gpsimd.tensor_tensor(ob[:], sres[:], xr[:], ALU.add).then_inc(ob_ok.sem, 1)
                    if nx2 and n == 4:
                        pool.wait_ge(*done(mv_ok, b + 2))
                        inv_root(r1[:], r1t[:], mv[:, :, 1], 1.0, r1_step, b + 2, 0, ((xn_ok, b + 1, None),))
                    if nx2 and n == 6:
                        pool.wait_ge(*done(r1_step, b + 2))
                        nc.gpsimd.tensor_tensor(vv[:], mv[:, :, 1], r1[:], ALU.mult).then_inc(r2_step.sem, 1)
                        pool.wait_ge(*done(r2_step, b + 2, 1))
                        nc.gpsimd.tensor_tensor(vvt[:], vv[:], r1[:], ALU.mult).then_inc(r2_step.sem, 1)
                        pool.wait_ge(*done(r2_step, b + 2, 2))
                        inv_root(r2[:], r2t[:], vvt[:], 1.0, r2_step, b + 2, 2, ((h0_ok, b + 1, None),))
                    if start(b, -2) and n == 10:
                        masks()
                        nc.gpsimd.memset(va[:], 0.0).then_inc(va_set.sem, 1)
                    if start(b, -1) and n == NCH:
                        nc.gpsimd.memset(kd[1][:].rearrange("p n t -> p (n t)").bitcast(F32), two_ones).then_inc(stacks_set.sem, 1)
                        nc.gpsimd.memset(qz[1][:], 0.0).then_inc(stacks_set.sem, 1)
                    if nx2 and n == 10:
                        pool.wait_ge(*done(sq_ok, b + 2))
                        inv_root(rs[:], sqm[:], sq[:], 1.0 / D, rs_step, b + 2, 0, ((nf_ok, b + 1, None),))
                if nx2:
                    for n, (parts, rest) in enumerate(((qp, qr), (kp, kr))):
                        pool.wait_ge(*done(qkr_ok, b + 2, n + 1))
                        apart(pool, b)
                        nc.gpsimd.tensor_scalar(parts[:, 1], rest[:], 1.0, 0.0, ALU.mult, ALU.add).then_inc(qkmid_ok.sem, 1)
                        pool.wait_ge(*done(qkmid_ok, b + 2, n + 1))
                        nc.gpsimd.tensor_tensor(parts[:, 2], rest[:], parts[:, 1], ALU.subtract).then_inc(qklo_ok.sem, 1)
                if main:
                    pool.wait_ge(*done(mv2_ok, b))
                    inv_root(r3[:], r3t[:], mv2[:, :, 1], 1.0, r3_step, b, 0, ((h2_ok, b - 1, None),))
                    pool.wait_ge(*done(r3_step, b))
                    pool.wait_ge(*done(h2T_ps, b - 1))
                    apart(pool, b)
                    for t in range(NT):
                        ts = nc.gpsimd.tensor_scalar(h2[:, t], x1[:, t], mv2[:, t, 0:1], r3[:, t:t + 1], ALU.subtract, ALU.mult)
                    ts.then_inc(h2_ok.sem, 1)
                    pool.wait_ge(*done(s_ok, b - 1))
                    nc.gpsimd.tensor_tensor(x1b[:], x1[:], rows["b2"][:].unsqueeze(1).to_broadcast([P, NT, D]), ALU.add).then_inc(x1b_ok.sem, 1)

            set_spare(pool, "pool_waited")
            schedule(pool, body)


_NAMES = {
    "x": "L0_attn_x", "ln1_g": "L0_attn_ln1_g", "ln1_b": "L0_attn_ln1_b", "WQ": "L0_attn_WQ", "bQ": "L0_attn_bQ",
    "WK": "L0_attn_WK", "bK": "L0_attn_bK", "WV": "L0_attn_WV", "bV": "L0_attn_bV", "WO": "L0_attn_WO",
    "bO": "L0_attn_bO", "Wg": "L0_attn_Wg", "bg": "L0_attn_bg", "A": "L0_attn_A", "Bw": "L0_attn_Bw",
    "Cw": "L0_attn_Cw", "ln2_g": "L0_attn_ln2_g", "ln2_b": "L0_attn_ln2_b", "W1": "L0_attn_W1", "b1": "L0_attn_b1",
    "W2": "L0_attn_W2", "b2": "L0_attn_b2", "norm_weight": "L0_ffn_norm_weight", "gate_weight": "L0_ffn_gate_weight",
    "gate_bias": "L0_ffn_gate_bias", "mlp1_weight": "L0_ffn_mlp1_weight", "mlp1_bias": "L0_ffn_mlp1_bias",
    "mlp2_weight": "L0_ffn_mlp2_weight", "mlp2_bias": "L0_ffn_mlp2_bias",
}


def kernel(**inputs):
    import concourse.bacc as bacc
    from concourse.bass_utils import run_bass_kernel_spmd as run

    nc = bacc.Bacc("TRN2", target_bir_lowering=False, num_devices=1)
    arrays, args = {}, {}
    for short, name in _NAMES.items():
        v = np.ascontiguousarray(inputs[name])
        arrays[name] = v
        args[short] = nc.dram_tensor(name, v.shape, mybir.dt.from_np(v.dtype), kind="ExternalInput").ap()
    out = nc.dram_tensor("out", (B, T, D), F32, kind="ExternalOutput").ap()
    build(nc, args, out)
    return run(nc, [arrays], core_ids=[0]).results[0]["out"]
```
